# Optimizing a Trainium2 kernel written in Bass

```python
import numpy as np
import jax
import jax.numpy as jnp

def _softmax(x, axis=-1):
    return jax.nn.softmax(x, axis=axis)
def _gelu(x):
    return jax.nn.gelu(x, approximate=True)
def _silu(x):
    return jax.nn.silu(x)
def _sigmoid(x):
    return jax.nn.sigmoid(x)
def _layernorm(x, axis=-1, eps=1e-5):
    m = jnp.mean(x, axis=axis, keepdims=True)
    v = jnp.var(x, axis=axis, keepdims=True)
    return (x - m) / jnp.sqrt(v + eps)
def _scatter_add(tgt, idx, src, axis=0):
    return tgt.at[idx].add(src)
def _segment_sum(src, seg, n):
    return jax.ops.segment_sum(src, seg, n)

kernel_name = 'mk_conv_seq_d2_conv_nhwc192_4528c9'

def setup_inputs(seed: int = 0):
    np.random.seed(seed)
    _w = jnp.asarray
    def _rec_inputs():
        import jax
        import jax.numpy as jnp
        _gk = jax.random.key(seed)
        x = -0.000357 + 1 * jax.random.normal(jax.random.fold_in(_gk, 1), (32, 56, 56, 192), jnp.float32)
        return x
    x = _rec_inputs()
    def _L0_conv_setup():
        import jax, jax.numpy as jnp
        import numpy as np
        from jax import lax

        def quick_gelu(x):
            return x * jax.nn.sigmoid(1.702 * x)
        key = jax.random.key(seed)
        ks = jax.random.split(key, 12)
        B, H, W, C, D, M = (32, 56, 56, 192, 64, 8)
        g = lambda k, shape, s: jax.random.normal(k, shape, jnp.float32) * s
        return {'x': jax.random.normal(ks[0], (B, H, W, C), jnp.float32), 'W1': g(ks[1], (64, C), 0.05), 'b1': jnp.zeros((64,), jnp.float32), 'W2': g(ks[2], (64, 64), 0.05), 'b2': jnp.zeros((64,), jnp.float32), 'mask_token': g(ks[3], (M, 64), 0.05), 'Wh': g(ks[4], (D * D * 9, 64), 0.02), 'bh': g(ks[5], (D * D * 9,), 0.02), 'Wd': g(ks[6], (D, C), 0.05), 'bd': jnp.zeros((D,), jnp.float32), 'Wu': g(ks[7], (C, D), 0.02), 'bu': jnp.zeros((C,), jnp.float32)}
    _L0_conv_all = _L0_conv_setup()
    _L0_conv_in = {k: v for k, v in _L0_conv_all.items() if k in ('W1', 'b1', 'W2', 'b2', 'mask_token', 'Wh', 'bh', 'Wd', 'bd', 'Wu', 'bu', )}
    del _L0_conv_all

    def _L1_conv_setup():
        import jax, jax.numpy as jnp
        import numpy as np
        from jax import lax
        B, H, W, C = (32, 56, 56, 192)
        EXPAND = 2
        D_INNER = C * EXPAND
        EPS = 1e-05

        def _forward(x, gamma, beta, sel_w1, sel_b1, sel_w2, sel_b2, fc1_w, fc1_b, dw_w, dw_b, fc2_w, fc2_b):
            b, h, w, c = x.shape
            mu = x.mean(-1, keepdims=True)
            var = ((x - mu) ** 2).mean(-1, keepdims=True)
            x_norm = (x - mu) / jnp.sqrt(var + EPS) * gamma + beta
            x_gray = x_norm.mean(-1)
            grad_h = jnp.abs(x_gray[:, :, 1:] - x_gray[:, :, :-1]).mean(axis=(1, 2))
            grad_v = jnp.abs(x_gray[:, 1:, :] - x_gray[:, :-1, :]).mean(axis=(1, 2))
            scores = jnp.stack([grad_h, grad_v, 0.8 * (grad_h + grad_v) * 0.5, jnp.abs(grad_h - grad_v)], axis=1)
            logits = jax.nn.relu(scores @ sel_w1 + sel_b1) @ sel_w2 + sel_b2
            probs = jax.nn.softmax(logits, axis=-1)
            idx = jnp.argmax(probs, axis=-1) % 4
            is_v = (idx == 1)[:, None, None, None]
            x_sel = jnp.where(is_v, jnp.swapaxes(x_norm, 1, 2), x_norm)
            seq = x_sel.reshape(b, h * w, c)
            t = seq @ fc1_w + fc1_b
            t = jnp.swapaxes(t, 1, 2)
            t = lax.conv_general_dilated(t, dw_w, window_strides=(1,), padding=((1, 1),), feature_group_count=D_INNER, dimension_numbers=('NCH', 'OIH', 'NCH')) + dw_b[None, :, None]
            t = jnp.swapaxes(t, 1, 2)
            t = jax.nn.gelu(t, approximate=False)
            out_seq = t @ fc2_w + fc2_b
            out = out_seq.reshape(b, h, w, c)
            return x + out
        key = jax.random.key(seed)
        ks = jax.random.split(key, 12)

        def init(k, shape, fan_in):
            return jax.random.normal(k, shape, dtype=jnp.float32) / np.sqrt(fan_in)
        return {'x': jax.random.normal(ks[0], (B, H, W, C), dtype=jnp.float32), 'gamma': jnp.ones((C,), jnp.float32), 'beta': jnp.zeros((C,), jnp.float32), 'sel_w1': init(ks[1], (4, 16), 4), 'sel_b1': jnp.zeros((16,), jnp.float32), 'sel_w2': init(ks[2], (16, 4), 16), 'sel_b2': jnp.zeros((4,), jnp.float32), 'fc1_w': init(ks[3], (C, D_INNER), C), 'fc1_b': jnp.zeros((D_INNER,), jnp.float32), 'dw_w': init(ks[4], (D_INNER, 1, 3), 3), 'dw_b': jnp.zeros((D_INNER,), jnp.float32), 'fc2_w': init(ks[5], (D_INNER, C), D_INNER), 'fc2_b': jnp.zeros((C,), jnp.float32)}
    _L1_conv_all = _L1_conv_setup()
    _L1_conv_in = {k: v for k, v in _L1_conv_all.items() if k in ('gamma', 'beta', 'sel_w1', 'sel_b1', 'sel_w2', 'sel_b2', 'fc1_w', 'fc1_b', 'dw_w', 'dw_b', 'fc2_w', 'fc2_b', )}
    del _L1_conv_all

    return {
        "x": x,
        "L0_conv_W1": _L0_conv_in["W1"],
        "L0_conv_b1": _L0_conv_in["b1"],
        "L0_conv_W2": _L0_conv_in["W2"],
        "L0_conv_b2": _L0_conv_in["b2"],
        "L0_conv_mask_token": _L0_conv_in["mask_token"],
        "L0_conv_Wh": _L0_conv_in["Wh"],
        "L0_conv_bh": _L0_conv_in["bh"],
        "L0_conv_Wd": _L0_conv_in["Wd"],
        "L0_conv_bd": _L0_conv_in["bd"],
        "L0_conv_Wu": _L0_conv_in["Wu"],
        "L0_conv_bu": _L0_conv_in["bu"],
        "L1_conv_gamma": _L1_conv_in["gamma"],
        "L1_conv_beta": _L1_conv_in["beta"],
        "L1_conv_sel_w1": _L1_conv_in["sel_w1"],
        "L1_conv_sel_b1": _L1_conv_in["sel_b1"],
        "L1_conv_sel_w2": _L1_conv_in["sel_w2"],
        "L1_conv_sel_b2": _L1_conv_in["sel_b2"],
        "L1_conv_fc1_w": _L1_conv_in["fc1_w"],
        "L1_conv_fc1_b": _L1_conv_in["fc1_b"],
        "L1_conv_dw_w": _L1_conv_in["dw_w"],
        "L1_conv_dw_b": _L1_conv_in["dw_b"],
        "L1_conv_fc2_w": _L1_conv_in["fc2_w"],
        "L1_conv_fc2_b": _L1_conv_in["fc2_b"],
    }

def reference(x, L0_conv_W1, L0_conv_b1, L0_conv_W2, L0_conv_b2, L0_conv_mask_token, L0_conv_Wh, L0_conv_bh, L0_conv_Wd, L0_conv_bd, L0_conv_Wu, L0_conv_bu, L1_conv_gamma, L1_conv_beta, L1_conv_sel_w1, L1_conv_sel_b1, L1_conv_sel_w2, L1_conv_sel_b2, L1_conv_fc1_w, L1_conv_fc1_b, L1_conv_dw_w, L1_conv_dw_b, L1_conv_fc2_w, L1_conv_fc2_b):
    import jax
    import jax.numpy as jnp
    def _L0_conv_ref(x, W1, b1, W2, b2, mask_token, Wh, bh, Wd, bd, Wu, bu):
        import jax, jax.numpy as jnp
        import numpy as np
        from jax import lax

        def quick_gelu(x):
            return x * jax.nn.sigmoid(1.702 * x)
        B, H, W_, C = x.shape
        D = Wd.shape[0]
        M = mask_token.shape[0]
        pf = jax.nn.relu(jnp.einsum('bhwc,kc->bhwk', x, W1) + b1)
        pf = jnp.einsum('bhwk,jk->bhwj', pf, W2) + b2
        mask = jnp.einsum('bhwk,mk->mbhw', pf, mask_token)
        mask = jax.nn.softmax(mask.reshape(M, B, -1), axis=-1).reshape(M, B, H, W_)
        mwf = (mask.sum(0)[..., None] * pf).sum(axis=(1, 2))
        conv_w = (jnp.einsum('bk,ok->bo', mwf, Wh) + bh).reshape(B, D, D, 3, 3)
        xd = jnp.einsum('bhwc,dc->bhwd', x, Wd) + bd
        xp = quick_gelu(xd.transpose(0, 3, 1, 2))

        def conv1(xi, wi):
            return lax.conv_general_dilated(xi[None], wi, (1, 1), [(1, 1), (1, 1)])[0]
        xc = jax.vmap(conv1)(xp, conv_w)
        xd2 = quick_gelu(xc.transpose(0, 2, 3, 1))
        xu = jnp.einsum('bhwd,cd->bhwc', xd2, Wu) + bu
        return xu + x

    def _L1_conv_ref(x, gamma, beta, sel_w1, sel_b1, sel_w2, sel_b2, fc1_w, fc1_b, dw_w, dw_b, fc2_w, fc2_b):
        import jax, jax.numpy as jnp
        import numpy as np
        from jax import lax
        B, H, W, C = (32, 56, 56, 192)
        EXPAND = 2
        D_INNER = C * EXPAND
        EPS = 1e-05

        def _forward(x, gamma, beta, sel_w1, sel_b1, sel_w2, sel_b2, fc1_w, fc1_b, dw_w, dw_b, fc2_w, fc2_b):
            b, h, w, c = x.shape
            mu = x.mean(-1, keepdims=True)
            var = ((x - mu) ** 2).mean(-1, keepdims=True)
            x_norm = (x - mu) / jnp.sqrt(var + EPS) * gamma + beta
            x_gray = x_norm.mean(-1)
            grad_h = jnp.abs(x_gray[:, :, 1:] - x_gray[:, :, :-1]).mean(axis=(1, 2))
            grad_v = jnp.abs(x_gray[:, 1:, :] - x_gray[:, :-1, :]).mean(axis=(1, 2))
            scores = jnp.stack([grad_h, grad_v, 0.8 * (grad_h + grad_v) * 0.5, jnp.abs(grad_h - grad_v)], axis=1)
            logits = jax.nn.relu(scores @ sel_w1 + sel_b1) @ sel_w2 + sel_b2
            probs = jax.nn.softmax(logits, axis=-1)
            idx = jnp.argmax(probs, axis=-1) % 4
            is_v = (idx == 1)[:, None, None, None]
            x_sel = jnp.where(is_v, jnp.swapaxes(x_norm, 1, 2), x_norm)
            seq = x_sel.reshape(b, h * w, c)
            t = seq @ fc1_w + fc1_b
            t = jnp.swapaxes(t, 1, 2)
            t = lax.conv_general_dilated(t, dw_w, window_strides=(1,), padding=((1, 1),), feature_group_count=D_INNER, dimension_numbers=('NCH', 'OIH', 'NCH')) + dw_b[None, :, None]
            t = jnp.swapaxes(t, 1, 2)
            t = jax.nn.gelu(t, approximate=False)
            out_seq = t @ fc2_w + fc2_b
            out = out_seq.reshape(b, h, w, c)
            return x + out
        return _forward(x, gamma, beta, sel_w1, sel_b1, sel_w2, sel_b2, fc1_w, fc1_b, dw_w, dw_b, fc2_w, fc2_b)

    def _gn(v, G=32, eps=1e-5):
        B_, H_, W_, C_ = v.shape
        g = v.reshape(B_, H_, W_, G, C_ // G)
        m = jnp.mean(g, axis=(1, 2, 4), keepdims=True)
        s = jnp.var(g, axis=(1, 2, 4), keepdims=True)
        return ((g - m) / jnp.sqrt(s + eps)).reshape(v.shape)

    def _ln_c(v, eps=1e-6):
        m = jnp.mean(v, axis=-1, keepdims=True)
        s = jnp.var(v, axis=-1, keepdims=True)
        return (v - m) / jnp.sqrt(s + eps)

    def _ln_t(v, eps=1e-5):
        m = jnp.mean(v, axis=-1, keepdims=True)
        s = jnp.var(v, axis=-1, keepdims=True)
        return (v - m) / jnp.sqrt(s + eps)

    def _to_tokens(v):
        B_, H_, W_, C_ = v.shape
        return v.reshape(B_, H_ * W_, C_)
    def _from_tokens(t, like):
        return t.reshape(like.shape)

    x = _L0_conv_ref(x, L0_conv_W1, L0_conv_b1, L0_conv_W2, L0_conv_b2, L0_conv_mask_token, L0_conv_Wh, L0_conv_bh, L0_conv_Wd, L0_conv_bd, L0_conv_Wu, L0_conv_bu)
    x = _L1_conv_ref(x, L1_conv_gamma, L1_conv_beta, L1_conv_sel_w1, L1_conv_sel_b1, L1_conv_sel_w2, L1_conv_sel_b2, L1_conv_fc1_w, L1_conv_fc1_b, L1_conv_dw_w, L1_conv_dw_b, L1_conv_fc2_w, L1_conv_fc2_b)
    return x


_drawn_inputs = setup_inputs


def setup_inputs(seed=0):
    import zlib

    import numpy as np

    out = dict(_drawn_inputs(seed))
    spreads = {'L0_conv_b1': (0.0, 0.285),
     'L0_conv_b2': (0.0, 0.1),
     'L0_conv_bd': (0.0, 0.1),
     'L0_conv_bu': (0.0, 0.1),
     'L1_conv_gamma': (1.0, 0.2),
     'L1_conv_beta': (0.0, 0.1),
     'L1_conv_sel_b1': (0.0, 0.1),
     'L1_conv_sel_b2': (0.0, 0.1),
     'L1_conv_fc1_b': (0.0, 0.1),
     'L1_conv_dw_b': (0.0, 0.1),
     'L1_conv_fc2_b': (0.0, 0.1)}
    factors = {'L0_conv_W1': 6.562, 'L0_conv_mask_token': 8.0, 'L0_conv_bh': 3.729}
    for name, (base, spread) in spreads.items():
        noise = np.random.default_rng([zlib.crc32(name.encode()), seed]).standard_normal(out[name].shape)
        drawn = base * np.exp(spread * noise) if base else spread * noise
        out[name] = jnp.asarray(drawn.astype(out[name].dtype))
    for name, factor in factors.items():
        out[name] = (out[name] * factor).astype(out[name].dtype)
    return out
```

```python
from contextlib import ExitStack

import concourse.bass as bass
from concourse import mybir

F32 = mybir.dt.float32
I32 = mybir.dt.int32
ALU = mybir.AluOpType
ACT = mybir.ActivationFunctionType
AX = mybir.AxisListType

B, H, W, C = 32, 56, 56, 192
D = 64
M = 8
DI = 384
NB = DI // 128
SEL = 16
PIX = H * W
GP = 2 * W
NG = PIX // GP
TG = 4
NT = NG // TG
TP = TG * GP
C1 = C - 128
PW = W + 2
PADDED = PW * PW
CR = 7
CT = H // 2 // CR
CP = CR * W
HP = PIX // 2
HG = NG // 2
YW = M + D
TAPW = 9 * D
OC = D * TAPW
WCH = 9 * 512
NCH = OC // WCH
XS = PIX + 2
EPS = 1e-5


def build(nc, t):
    ctx = ExitStack()
    with ctx:
        def sem(name):
            return ctx.enter_context(nc.semaphore(name))

        def keep(name, shape, dt=F32):
            return ctx.enter_context(nc.sbuf_tensor(name, shape, dt))

        k = {}
        k["ident"] = keep("ident", [128, 128])
        k["w_ad"] = keep("w_ad", [128, 2, 128])
        k["bias_ad"] = keep("bias_ad", [128, 1])
        k["floor_ad"] = keep("floor_ad", [128, 1])
        k["pick"] = keep("pick", [128, YW])
        k["w2raw"] = keep("w2raw", [D, D])
        k["tokT"] = keep("tokT", [D, M])
        k["w2T"] = keep("w2T", [D + 1, D])
        k["ones"] = keep("ones", [M, 112])
        k["pooled"] = keep("pooled", [D + 1, B])
        k["mwf"] = keep("mwf", [D + 1, B])
        k["wu"] = keep("wu", [128, 2 * C])
        k["fc1"] = keep("fc1", [128, 2, DI])
        k["gamma_c"] = keep("gamma_c", [128, 2])
        k["beta_c"] = keep("beta_c", [128, 2])
        k["fc1_b"] = keep("fc1_b", [128, NB])
        k["dw"] = keep("dw", [128, NB, 3])
        k["dw_b"] = keep("dw_b", [128, NB])
        k["bias3"] = keep("bias3", [128, 3, NB])
        k["tmp3"] = keep("tmp3", [128, 2, NB])
        k["fc2"] = keep("fc2", [128, NB, C])
        k["gamma_r"] = keep("gamma_r", [GP, C])
        k["gamma_sum"] = keep("gamma_sum", [GP, 1])
        k["bu_r"] = keep("bu_r", [GP, C])
        k["fc2b_r"] = keep("fc2b_r", [GP, C])
        k["diff"] = keep("diff", [GP, 4, GP])
        k["mixs"] = keep("mixs", [GP, 2, 4])
        k["sel_w1"] = keep("sel_w1", [4, 128])
        k["sel_b1"] = keep("sel_b1", [128, 1])
        k["sel_w2"] = keep("sel_w2", [128, 4])
        k["sel_b2"] = keep("sel_b2", [1, 4])
        k["expo"] = keep("expo", [GP, NG])

        setup(nc, t, k, sem)
        pass_one(nc, t, k, sem)
        conv_weights(nc, t, k, sem)
        pass_two(nc, t, k, sem)


def at(i, per, n):
    return i * per + n


def wait(eng, s, i, per, n):
    v = i * per + n
    if isinstance(v, int) and v <= 0:
        return
    eng.wait_ge(s, v)


def alone(eng, s):
    eng.sem_inc(s, 1)


def setup(nc, t, k, sem):
    loads = [
        ("ident", k["ident"][:, :]), ("diff", k["diff"][:, :, :]), ("mixs", k["mixs"][:, :, :]),
        ("WdT0", k["w_ad"][:, 0, 0:D]), ("W1T0", k["w_ad"][:, 0, D:128]),
        ("WdT1", k["w_ad"][0:C1, 1, 0:D]), ("W1T1", k["w_ad"][0:C1, 1, D:128]),
        ("bd", k["bias_ad"][0:D, :]), ("b1", k["bias_ad"][D:128, :]),
        ("W2", k["w2raw"][:, :]), ("tokT", k["tokT"][:, :]),
        ("W2T", k["w2T"][0:D, :]), ("b2", k["w2T"][D:D + 1, :]),
        ("WuT", k["wu"][0:D, 0:C]), ("WuT", k["wu"][D:128, C:2 * C]),
        ("fc1_0", k["fc1"][:, 0, :]), ("fc1_1", k["fc1"][0:C1, 1, :]),
        ("gamma0", k["gamma_c"][:, 0:1]), ("gamma1", k["gamma_c"][0:C1, 1:2]),
        ("beta0", k["beta_c"][:, 0:1]), ("beta1", k["beta_c"][0:C1, 1:2]),
        ("fc1_b", k["fc1_b"][:, :]), ("dw_w", k["dw"][:, :, :]), ("dw_b", k["dw_b"][:, :]),
        ("fc2_w", k["fc2"][:, :, :]),
        ("sel_w1", k["sel_w1"][:, 0:SEL]), ("sel_b1", k["sel_b1"][0:SEL, :]),
        ("sel_w2", k["sel_w2"][0:SEL, :]), ("sel_b2", k["sel_b2"][:, :]),
    ]
    rows = [("gamma", k["gamma_r"]), ("bu", k["bu_r"]), ("fc2_b", k["fc2b_r"])]
    weights_in, zeroed, small_mm, chain = sem("weights_in"), sem("zeroed"), sem("small_mm"), sem("chain")
    total = 16 * (len(loads) + len(rows))
    with nc.psum_tensor("ps_tok", [128, M], F32) as ps_tok, \
            nc.psum_tensor("ps_beta", [128, NB, 1], F32) as ps_beta, nc.Block() as block:

        @block.sync
        def _(sp):
            sp.wait_ge(zeroed, 8)
            for name, dst in loads:
                sp.dma_start(dst, t[name]).then_inc(weights_in, 16)
            for name, dst in rows:
                sp.dma_start(dst[:, :], t[name].to_broadcast([GP, C])).then_inc(weights_in, 16)

        @block.vector
        def _(dve):
            dve.memset(k["w_ad"][:, 1, :], 0.0).then_inc(zeroed, 1)
            dve.memset(k["wu"][:, :], 0.0).then_inc(zeroed, 1)
            dve.memset(k["fc1"][:, 1, :], 0.0).then_inc(zeroed, 1)
            dve.memset(k["gamma_c"][:, :], 0.0).then_inc(zeroed, 1)
            dve.memset(k["beta_c"][:, :], 0.0).then_inc(zeroed, 1)
            dve.memset(k["sel_w1"][:, :], 0.0).then_inc(zeroed, 1)
            dve.memset(k["sel_b1"][:, :], 0.0).then_inc(zeroed, 1)
            dve.memset(k["sel_w2"][:, :], 0.0).then_inc(zeroed, 1)
            dve.memset(k["pick"][0:D, :], 0.0)
            dve.memset(k["floor_ad"][0:D, :], -3.0e38)
            dve.memset(k["floor_ad"][D:128, :], 0.0)
            dve.memset(k["ones"][:, :], 1.0)
            dve.memset(k["mwf"][D:D + 1, :], 1.0)
            dve.memset(k["expo"][:, :], -0.5)
            dve.wait_ge(weights_in, total)
            dve.wait_ge(small_mm, 1)
            dve.tensor_copy(k["pick"][D:128, 0:M], ps_tok[D:128, :])
            dve.tensor_copy(k["pick"][D:128, M:YW], k["ident"][D:128, D:128])
            dve.tensor_scalar(k["wu"][:, :], k["wu"][:, :], 0.25, None, ALU.mult)
            for c in range(2):
                dve.tensor_scalar(k["fc1"][:, c, :], k["fc1"][:, c, :], k["gamma_c"][:, c:c + 1], None, ALU.mult)
            dve.reduce_sum(k["gamma_sum"][:, :], k["gamma_r"][:, :], AX.X)
            bp, ws = k["tmp3"][:, 0, :], k["tmp3"][:, 1, :]
            dve.tensor_tensor(bp, ps_beta[:, :, 0], k["fc1_b"][:, :], ALU.add)
            dve.tensor_tensor(ws, k["dw"][:, :, 0], k["dw"][:, :, 1], ALU.add).then_inc(chain, 1)
            dve.wait_ge(chain, 1)
            dve.tensor_tensor(ws, ws, k["dw"][:, :, 2], ALU.add).then_inc(chain, 1)
            dve.wait_ge(chain, 2)
            dve.tensor_tensor(ws, ws, bp, ALU.mult).then_inc(chain, 1)
            dve.wait_ge(chain, 3)
            dve.tensor_tensor(k["bias3"][:, 0, :], ws, k["dw_b"][:, :], ALU.add).then_inc(chain, 1)
            dve.wait_ge(chain, 4)
            dve.tensor_tensor(ws, k["dw"][:, :, 0], bp, ALU.mult).then_inc(chain, 1)
            dve.wait_ge(chain, 5)
            dve.tensor_tensor(k["bias3"][:, 1, :], k["bias3"][:, 0, :], ws, ALU.subtract).then_inc(chain, 1)
            dve.wait_ge(chain, 6)
            dve.tensor_tensor(ws, k["dw"][:, :, 2], bp, ALU.mult).then_inc(chain, 1)
            dve.wait_ge(chain, 7)
            dve.tensor_tensor(k["bias3"][:, 2, :], k["bias3"][:, 0, :], ws, ALU.subtract).then_inc(chain, 1)

        @block.tensor
        def _(pe):
            pe.wait_ge(weights_in, total)
            pe.matmul(ps_tok[D:128, :], k["w2raw"][:, :], k["tokT"][:, :], start=True, stop=True)
            for m in range(NB):
                for c in range(2):
                    mm = pe.matmul(ps_beta[:, m, :], k["fc1"][:, c, m * 128:(m + 1) * 128],
                                   k["beta_c"][:, c:c + 1], start=(c == 0), stop=(c == 1))
            mm.then_inc(small_mm, 1)


def pass_one(nc, t, k, sem):
    x_v, map_v = t["x_g"], t["map"]
    with ExitStack() as ctx:
        def sb(name, shape):
            return ctx.enter_context(nc.sbuf_tensor(name, shape, F32))

        def ps(name, shape):
            return ctx.enter_context(nc.psum_tensor(name, shape, F32))

        xa = sb("xa", [GP, 2, NG, C])
        xT = sb("xT", [128, 2, 2, TP])
        y = sb("y", [128, 2, TP])
        th = sb("th", [D, 2, TP])
        pad = sb("pad", [D, 2, PADDED])
        yl = sb("yl", [GP, 2, NG, YW + 1])
        mx = sb("mx", [GP, M])
        mx8 = sb("mx8", [M, 1])
        dg = sb("dg", [M, M])
        lg = sb("lg", [GP, NG, M])
        ex = sb("ex", [GP, NG, M])
        rz = sb("rz", [M, 1])
        pn = sb("pn", [M, D + 1])
        ps_c0 = ps("ps_c0", [128, 2, 512])
        ps_c1 = ps("ps_c1", [128, 1, 512])
        ps_a = ps("ps_a", [128, 2, 512])
        ps_y = ps("ps_y", [128, 2, 512])
        ps_q = ps("ps_q", [128, 512])
        x_in = [sem("x_in0"), sem("x_in1")]
        turned, c0_out, c1_out = sem("turned"), sem("c0_out"), sem("c1_out")
        proj, y_ready, th_ready, map_ready = sem("proj"), sem("y_ready"), sem("th_ready"), sem("map_ready")
        picked, yl_ready = sem("picked"), sem("yl_ready")
        map_out = [sem("map_out0"), sem("map_out1")]
        q_max, q_turn, q_m8, q_diag, q_bc, q_sub, q_exp = (sem("q_" + n) for n in ("max", "turn", "m8", "diag", "bc", "sub", "exp"))
        q_pool, q_rz, q_norm, q_sum, q_done = (sem("q_" + n) for n in ("pool", "rz", "norm", "sum", "done"))
        border = sem("border")
        block = ctx.enter_context(nc.Block())
        ident = k["ident"]

        def schedule(eng, features, pool):
            features(0, 0, None)
            features(1, 1, 0)
            with eng.Fori(2, B - 1, 2) as i:
                features(i, 0, 1)
                features(i + 1, 1, 0)
            for slot in range(NT):
                pool(B - 1, 1, slot)

        @block.sync
        def _(sp):
            sp.dma_start(xa[:, 0, :, :], x_v[0]).then_inc(x_in[0], 16)
            sp.dma_start(xa[:, 1, :, :], x_v[1]).then_inc(x_in[1], 16)

            def step(i, p, more):
                if more:
                    sp.wait_ge(turned, at(i, NT, NT))
                    sp.dma_start(xa[:, p, :, :], x_v[i + 2]).then_inc(x_in[p], 16)
                sp.wait_ge(map_ready, at(i, NT, NT))
                sp.dma_start(map_v[i], pad[:, p, :]).then_inc(map_out[p], 16)

            with sp.Fori(0, B - 3, 2) as i:
                step(i, 0, True)
                step(i + 1, 1, True)
            step(B - 2, 0, False)
            step(B - 1, 1, False)
            for p in range(2):
                sp.wait_ge(map_out[p], 16 * B // 2)

        @block.tensor
        def _(pe):
            def turn(i, p, n):
                if n == 0:
                    pe.wait_ge(x_in[p], (i - p) * 8 + 16)
                wait(pe, c1_out, i, NT, n)
                wait(pe, c0_out, i, NT, n - 1)
                for g in range(TG):
                    pe.transpose(ps_c0[:, n_par(i, p, n), g * GP:(g + 1) * GP], xa[:, p, n * TG + g, 0:128], ident[0:GP, 0:GP])
                for g in range(TG):
                    tr = pe.transpose(ps_c1[0:C1, 0, g * GP:(g + 1) * GP], xa[:, p, n * TG + g, 128:C], ident[0:GP, 0:GP])
                tr.then_inc(turned, 1)

            def project(i, p, n):
                r = n_par(i, p, n)
                pe.wait_ge(c0_out, at(i, NT, n + 1))
                pe.wait_ge(c1_out, at(i, NT, n + 1))
                wait(pe, y_ready, i, NT, n - 1)
                for c in range(2):
                    mm = pe.matmul(ps_a[:, r, 0:TP], k["w_ad"][:, c, :], xT[:, r, c, :], start=(c == 0), stop=(c == 1))
                mm.then_inc(proj, 1)

            def pick(i, p, n):
                r = n_par(i, p, n)
                pe.wait_ge(y_ready, at(i, NT, n + 1))
                wait(pe, yl_ready, i, NT, n - 1)
                for g in range(TG):
                    mm = pe.matmul(ps_y[0:GP, r, g * YW:(g + 1) * YW], y[:, r, g * GP:(g + 1) * GP], k["pick"][:, :], start=True, stop=True)
                mm.then_inc(picked, 1)

            def pool(i, p, slot):
                if slot == 0:
                    pe.wait_ge(q_max, at(i, 1, 1))
                    pe.transpose(ps_q[0:M, 0:GP], mx[:, :], ident[0:GP, 0:GP]).then_inc(q_turn, 1)
                if slot == 1:
                    pe.wait_ge(q_diag, at(i, 1, 1))
                    pe.matmul(ps_q[0:GP, 128:128 + M], k["ones"][:, :], dg[:, :], start=True, stop=True).then_inc(q_bc, 1)
                if slot == 3:
                    pe.wait_ge(q_exp, at(i, 1, 1))
                    for g in range(NG):
                        mm = pe.matmul(ps_q[0:M, 160:160 + D + 1], ex[:, g, :], yl[:, p, g, M:YW + 1], start=(g == 0), stop=(g == NG - 1))
                    mm.then_inc(q_pool, 1)
                if slot == 5:
                    pe.wait_ge(q_norm, at(i, 1, 1))
                    pe.matmul(ps_q[0:D + 1, 256:257], pn[:, :], k["ones"][:, 0:1], start=True, stop=True).then_inc(q_sum, 1)

            def features(i, p, q):
                for n in range(NT + 2):
                    if n < NT:
                        turn(i, p, n)
                    if 1 <= n <= NT:
                        project(i, p, n - 1)
                    if n >= 2:
                        pick(i, p, n - 2)
                        if q is not None:
                            pool(i - 1, q, n - 2)

            schedule(pe, features, pool)

        @block.scalar
        def _(act):
            def evac_c0(i, p, n):
                r = n_par(i, p, n)
                act.wait_ge(turned, at(i, NT, n + 1))
                wait(act, proj, i, NT, n - 1)
                act.activation(xT[:, r, 0, :], ps_c0[:, r, 0:TP], ACT.Copy).then_inc(c0_out, 1)

            def tanh(i, p, n):
                r = n_par(i, p, n)
                act.wait_ge(y_ready, at(i, NT, n + 1))
                wait(act, map_ready, i, NT, n - 1)
                act.activation(th[:, r, :], y[0:D, r, :], ACT.Tanh, scale=0.851).then_inc(th_ready, 1)

            def evac_y(i, p, n):
                r = n_par(i, p, n)
                act.wait_ge(picked, at(i, NT, n + 1))
                if n == 0:
                    wait(act, q_pool, i, 1, -1)
                act.activation(yl[:, p, n * TG:(n + 1) * TG, 0:YW],
                               ps_y[0:GP, r, 0:TG * YW].rearrange("p (g w) -> p g w", w=YW), ACT.Copy).then_inc(yl_ready, 1)

            def pool(i, p, slot):
                if slot == 2:
                    act.wait_ge(q_sub, at(i, 1, 1))
                    wait(act, q_pool, i, 1, 0)
                    act.activation(ex[:, :, :], lg[:, :, :], ACT.Exp).then_inc(q_exp, 1)

            def features(i, p, q):
                for n in range(NT + 2):
                    if n < NT:
                        evac_c0(i, p, n)
                    if 1 <= n <= NT:
                        tanh(i, p, n - 1)
                    if n >= 2:
                        evac_y(i, p, n - 2)
                        if q is not None:
                            pool(i - 1, q, n - 2)

            schedule(act, features, pool)

        @block.vector
        def _(dve):
            dve.memset(xT[64:128, :, 1, :], 0.0).then_inc(border, 1)
            dve.memset(pad[:, :, :], 0.0).then_inc(border, 1)
            dve.memset(yl[:, :, :, YW:YW + 1], 1.0).then_inc(border, 1)
            dve.wait_ge(border, 3)

            def evac_c1(i, p, n):
                r = n_par(i, p, n)
                dve.wait_ge(turned, at(i, NT, n + 1))
                wait(dve, proj, i, NT, n - 1)
                dve.tensor_copy(xT[0:C1, r, 1, :], ps_c1[0:C1, 0, 0:TP]).then_inc(c1_out, 1)

            def biased(i, p, n):
                r = n_par(i, p, n)
                dve.wait_ge(proj, at(i, NT, n + 1))
                wait(dve, picked, i, NT, n - 1)
                wait(dve, th_ready, i, NT, n - 1)
                wait(dve, map_ready, i, NT, n - 1)
                dve.tensor_scalar(y[:, r, :], ps_a[:, r, 0:TP], k["bias_ad"][:, :], k["floor_ad"][:, :],
                                  ALU.add, ALU.max).then_inc(y_ready, 1)

            def gelu_map(i, p, n):
                r = n_par(i, p, n)
                dve.wait_ge(th_ready, at(i, NT, n + 1))
                if n == 0 and not (isinstance(i, int) and i < 2):
                    dve.wait_ge(map_out[p], (i - p) * 8)
                rows = pad[:, p, PW + n * (TP // W) * PW:PW + (n + 1) * (TP // W) * PW].rearrange("c (h w) -> c h w", w=PW)
                dve.scalar_tensor_tensor(rows[:, :, 1:W + 1], th[:, r, :].rearrange("c (h w) -> c h w", w=W), 1.0,
                                         y[0:D, r, :].rearrange("c (h w) -> c h w", w=W), ALU.add, ALU.mult).then_inc(map_ready, 1)

            def pool(i, p, slot):
                if slot == 0:
                    dve.wait_ge(yl_ready, at(i, NT, NT))
                    wait(dve, q_turn, i, 1, 0)
                    dve.tensor_reduce(mx[:, :], yl[:, p, :, 0:M].rearrange("p g m -> p m g"), AX.X, ALU.max).then_inc(q_max, 1)
                    dve.wait_ge(q_turn, at(i, 1, 1))
                    dve.tensor_reduce(mx8[:, :], ps_q[0:M, 0:GP], AX.X, ALU.max).then_inc(q_m8, 1)
                    dve.wait_ge(q_m8, at(i, 1, 1))
                    dve.tensor_scalar(dg[:, :], ident[0:M, 0:M], mx8[:, :], None, ALU.mult).then_inc(q_diag, 1)
                if slot == 1:
                    dve.wait_ge(q_bc, at(i, 1, 1))
                    dve.tensor_tensor(lg[:, :, :].rearrange("p g m -> p m g"), yl[:, p, :, 0:M].rearrange("p g m -> p m g"),
                                      ps_q[0:GP, 128:128 + M].unsqueeze(2).to_broadcast([GP, M, NG]), ALU.subtract).then_inc(q_sub, 1)
                if slot == 4:
                    dve.wait_ge(q_pool, at(i, 1, 1))
                    dve.reciprocal(rz[:, :], ps_q[0:M, 160 + D:161 + D]).then_inc(q_rz, 1)
                    dve.wait_ge(q_rz, at(i, 1, 1))
                    dve.tensor_scalar(pn[:, :], ps_q[0:M, 160:161 + D], rz[:, :], None, ALU.mult).then_inc(q_norm, 1)
                if slot == 6:
                    dve.wait_ge(q_sum, at(i, 1, 1))
                    dve.tensor_copy(k["pooled"][:, bass.ds(i, 1)], ps_q[0:D + 1, 256:257]).then_inc(q_done, 1)

            def features(i, p, q):
                for n in range(NT + 2):
                    if n < NT:
                        evac_c1(i, p, n)
                    if 1 <= n <= NT:
                        biased(i, p, n - 1)
                    if n >= 2:
                        gelu_map(i, p, n - 2)
                        if q is not None:
                            pool(i - 1, q, n - 2)

            schedule(dve, features, pool)


def n_par(i, p, n):
    return (p * NT + n) % 2


def conv_weights(nc, t, k, sem):
    with ExitStack() as ctx:
        wh = ctx.enter_context(nc.sbuf_tensor("wh", [D + 1, 2, WCH], F32))
        cwo = ctx.enter_context(nc.sbuf_tensor("cwo", [B, 2, WCH], F32))
        ps_m = ctx.enter_context(nc.psum_tensor("ps_m", [128, 512], F32))
        ps_h = ctx.enter_context(nc.psum_tensor("ps_h", [128, 4, 512], F32))
        wh_in = [sem("wh_in0"), sem("wh_in1")]
        mwf_mm, mwf_ready, hyper, hyper_out = (sem(n) for n in ("mwf_mm", "mwf_ready", "hyper", "hyper_out"))
        cw_out = [sem("cw_out0"), sem("cw_out1")]
        N = WCH // 512
        block = ctx.enter_context(nc.Block())

        @block.sync
        def _(sp):
            for j in range(NCH + 2):
                if j < NCH:
                    if j >= 2:
                        sp.wait_ge(hyper, N * (j - 1))
                    sp.dma_start(wh[0:D, j % 2, :], t["WhT"][:, j * WCH:(j + 1) * WCH]).then_inc(wh_in[j % 2], 16)
                    sp.dma_start(wh[D:D + 1, j % 2, :], t["bh"][:, j * WCH:(j + 1) * WCH]).then_inc(wh_in[j % 2], 16)
                if j >= 2:
                    sp.wait_ge(hyper_out, N * (j - 1))
                    sp.dma_start(t["cw"][:, (j - 2) * WCH:(j - 1) * WCH], cwo[:, j % 2, :]).then_inc(cw_out[j % 2], 16)
            for r in range(2):
                sp.wait_ge(cw_out[r], 16 * NCH // 2)

        @block.tensor
        def _(pe):
            pe.matmul(ps_m[0:D, 0:B], k["w2T"][:, :], k["pooled"][:, :], start=True, stop=True).then_inc(mwf_mm, 1)
            pe.wait_ge(mwf_ready, 1)
            for j in range(NCH):
                pe.wait_ge(wh_in[j % 2], 32 * (j // 2 + 1))
                for n in range(N):
                    s = j * N + n
                    if s >= 4:
                        pe.wait_ge(hyper_out, s - 3)
                    pe.matmul(ps_h[0:B, s % 4, :], k["mwf"][:, :], wh[:, j % 2, n * 512:(n + 1) * 512],
                              start=True, stop=True).then_inc(hyper, 1)

        @block.vector
        def _(dve):
            dve.wait_ge(mwf_mm, 1)
            dve.tensor_copy(k["mwf"][0:D, :], ps_m[0:D, 0:B]).then_inc(mwf_ready, 1)
            for j in range(NCH):
                if j >= 2:
                    dve.wait_ge(cw_out[j % 2], 16 * (j // 2))
                for n in range(N):
                    s = j * N + n
                    dve.wait_ge(hyper, s + 1)
                    dve.tensor_copy(cwo[:, j % 2, n * 512:(n + 1) * 512], ps_h[0:B, s % 4, :]).then_inc(hyper_out, 1)


def pass_two(nc, t, k, sem):
    x_v, map_v, cw_v, out_v = t["x_g"], t["map"], t["cw_i"], t["out_g"]
    with ExitStack() as ctx:
        def sb(name, shape, dt=F32):
            return ctx.enter_context(nc.sbuf_tensor(name, shape, dt))

        def ps(name, shape):
            return ctx.enter_context(nc.psum_tensor(name, shape, F32))

        xin = sb("xin", [GP, NG, C])
        x1 = sb("x1", [GP, 2, NG, C])
        pads = sb("pads", [128, 2, PADDED])
        cw = sb("cw_s", [128, 2, 6, D])
        tc = sb("tc", [128, 2, CP])
        xd2 = sb("xd2", [128, HP])
        st = sb("st", [GP, NG, 6])
        gs = sb("gs", [GP, NG])
        junk = sb("junk", [GP, 2, C])
        m_s, m_d, m_v, m_q, var = (sb(n, [GP, NG]) for n in ("m_s", "m_d", "m_v", "m_q", "var"))
        rstd = sb("rstd", [GP, 2, NG])
        nmr = sb("nmr", [GP, 2, NG])
        gr1 = sb("gr1", [GP, NG])
        gray = sb("gray", [GP, NG])
        absd = sb("absd", [GP, 2, 2 * NG])
        hv = sb("hv", [GP, 2])
        sc4 = sb("sc4", [4, 1])
        hid = sb("hid", [128, 1])
        lgt = sb("lgt", [1, 4])
        cmp = sb("cmp", [1, 4])
        flag = sb("flag", [1, 2], I32)
        xh = sb("xh", [GP, 2, TG, C])
        seq = sb("seq", [128, 2, 2, XS])
        u = sb("u", [128, 2, NB, TP])
        gl = sb("gl", [128, 2, NB, TP])
        ps_x = ps("ps_x", [128, 2, 512])
        ps_o = ps("ps_o", [128, 2, 512])
        ps_f = ps("ps_f", [128, NB, 512])
        ps_s = ps("ps_s", [128, 512])
        s = {n: sem("t_" + n) for n in (
            "xin", "xb", "conv", "th", "xd", "wu", "x1", "sg", "st", "var", "rstd", "nmr", "gr1", "gray",
            "p1", "hv", "p2", "sc4", "p3", "hid", "p4", "l1", "l2", "flag", "xh", "x1b", "turn", "t0", "t1",
            "perm", "f1", "u", "w", "v", "g", "f2", "o", "zero", "vcopy", "pool_past", "pe_past")}
        cin = [sem("cin0"), sem("cin1")]
        outs = [sem("outs0"), sem("outs1")]
        block = ctx.enter_context(nc.Block())
        ident = k["ident"]

        def schedule(eng, local, select, mixer):
            local(0, 0)
            for piece in range(4):
                select(0, 0, piece)
            local(1, 1)
            mixer(0, 0, 1)
            with eng.Fori(1, B - 2, 2) as i:
                local(i + 1, 0)
                mixer(i, 1, i + 1)
                local(i + 2, 1)
                mixer(i + 1, 0, i + 2)
            mixer(B - 1, 1, None)

        @block.sync
        def _(sp):
            def load_conv(i, p):
                sp.dma_start(pads[0:D, p, :], map_v[i]).then_inc(cin[p], 16)
                sp.dma_start(pads[D:128, p, 0:PADDED - PW], map_v[i][:, PW:PADDED]).then_inc(cin[p], 16)
                sp.dma_start(cw[0:D, p, 0:3, :], cw_v[i][:, 0:3, :]).then_inc(cin[p], 16)
                sp.dma_start(cw[D:128, p, :, :], cw_v[i][:, 3:9, :]).then_inc(cin[p], 16)

            def load_x(i):
                sp.dma_start(xin[:, :, :], x_v[i]).then_inc(s["xin"], 16)

            def prefetch(i, p, x_next, conv_next):
                if x_next:
                    sp.wait_ge(s["x1"], at(i, HG, HG))
                    load_x(i + 1)
                if conv_next:
                    sp.wait_ge(s["conv"], at(i, CT, CT))
                    load_conv(i + 2, p)

            def store(i, p):
                for n in range(NT):
                    sp.wait_ge(s["o"], at(i, 2 * NT, 2 * n + 2))
                    sp.dma_start(out_v[i][:, n * TG:(n + 1) * TG, :], x1[:, p, n * TG:(n + 1) * TG, :]).then_inc(outs[p], 16)

            sp.wait_ge(s["zero"], 1)
            load_conv(0, 0)
            load_conv(1, 1)
            load_x(0)
            prefetch(0, 0, True, True)
            prefetch(1, 1, True, True)
            store(0, 0)
            with sp.Fori(1, B - 4, 2) as i:
                prefetch(i + 1, 0, True, True)
                store(i, 1)
                prefetch(i + 2, 1, True, True)
                store(i + 1, 0)
            prefetch(B - 2, 0, True, False)
            store(B - 3, 1)
            store(B - 2, 0)
            store(B - 1, 1)
            for p in range(2):
                sp.wait_ge(outs[p], 16 * NT * B // 2)

        @block.gpsimd
        def _(pool):
            def local(i, p):
                pool.wait_ge(s["xin"], at(i, 16, 16))
                pool.tensor_tensor(xin[:, :, :], xin[:, :, :], k["bu_r"][:, :].unsqueeze(1).to_broadcast([GP, NG, C]),
                                   ALU.add).then_inc(s["xb"], 1)
                pool.wait_ge(s["var"], at(i, 1, 1))
                wait(pool, s["xh"], i, NT, -NT)
                pool.tensor_tensor(rstd[:, p, :], var[:, :], k["expo"][:, :], ALU.pow).then_inc(s["rstd"], 1)

            def mixer(i, p, nxt):
                pool.wait_ge(s["nmr"], at(i, 1, 1))
                for n in range(NT):
                    r = n_par(i, p, n)
                    wait(pool, s["turn"], i, NT, n - 1)
                    alone(pool, s["pool_past"])
                    for g in range(TG):
                        c = n * TG + g
                        op = pool.tensor_scalar(xh[:, r, g, :], x1[:, p, c, :], rstd[:, p, c:c + 1], nmr[:, p, c:c + 1],
                                                ALU.mult, ALU.add)
                    op.then_inc(s["xh"], 1)
                pool.wait_ge(s["xh"], at(i, NT, NT))
                pool.tensor_tensor(x1[:, p, :, :], x1[:, p, :, :], k["fc2b_r"][:, :].unsqueeze(1).to_broadcast([GP, NG, C]),
                                   ALU.add).then_inc(s["x1b"], 1)
                pool.wait_ge(s["flag"], at(i, 1, 1))
                alone(pool, s["pool_past"])
                by_column = pool.value_load(flag[0:1, p:p + 1], min_val=0, max_val=1)
                pool.wait_ge(s["t0"], at(i, NT, NT))
                pool.wait_ge(s["t1"], at(i, NT, NT))
                alone(pool, s["pool_past"])
                with pool.If(by_column):
                    for c, rows in ((0, 128), (1, C1)):
                        pool.tensor_copy(seq[0:rows, 1, c, 1:1 + PIX].rearrange("c (w h) -> c w h", h=H),
                                         seq[0:rows, 0, c, 1:1 + PIX].rearrange("c (h w) -> c w h", w=W)).then_inc(s["vcopy"], 1)
                with pool.Else():
                    pool.nop().then_inc(s["vcopy"], 2)
                pool.wait_ge(s["vcopy"], at(i, 2, 2))
                pool.nop().then_inc(s["perm"], 1)

            schedule(pool, local, lambda i, p, piece: None, mixer)

        @block.tensor
        def _(pe):
            pe.wait_ge(s["zero"], 1)

            def local(i, p):
                pe.wait_ge(cin[p], (i - p) * 32 + 64)
                for n in range(CT):
                    wait(pe, s["xd"], i, CT, n - 1)
                    for tap in range(6):
                        down = tap // 3
                        for half in range(2):
                            o = (half * H // 2 + n * CR + down) * PW
                            mv = pads[:, p, o:o + CR * PW].rearrange("c (h w) -> c h w", w=PW)[:, :, tap % 3:tap % 3 + W]
                            mm = pe.matmul(ps_x[half * D:(half + 1) * D, n % 2, 0:CP], cw[:, p, tap, :], mv,
                                           start=(tap == 0), stop=(tap == 5))
                    mm.then_inc(s["conv"], 1)
                for g in range(HG):
                    pe.wait_ge(s["xd"], at(i, CT, (g * GP + GP - 1) // CP + 1))
                    if g < 2:
                        wait(pe, s["o"], i, 2 * NT, -2 * NT)
                    wait(pe, s["x1"], i, HG, g - 1)
                    pe.matmul(ps_o[0:GP, g % 2, 0:2 * C], xd2[:, g * GP:(g + 1) * GP], k["wu"][:, :],
                              start=True, stop=True).then_inc(s["wu"], 1)

            def select(i, p, piece):
                if piece == 0:
                    pe.wait_ge(s["gray"], at(i, 1, 1))
                    pe.matmul(ps_s[0:GP, 0:NG], k["diff"][:, 0, :], gray[:, :], start=True, stop=True)
                    pe.matmul(ps_s[0:GP, NG:2 * NG], k["diff"][:, 1, :], gray[:, :], start=True, stop=True)
                    pe.matmul(ps_s[0:GP, 2 * NG:3 * NG - 1], k["diff"][:, 2, :], gray[:, 0:NG - 1], start=True, stop=False)
                    pe.matmul(ps_s[0:GP, 2 * NG:3 * NG - 1], k["diff"][:, 3, :], gray[:, 1:NG], start=False, stop=True).then_inc(s["p1"], 1)
                if piece == 1:
                    pe.wait_ge(s["hv"], at(i, 1, 1))
                    pe.matmul(ps_s[0:4, 100:101], k["mixs"][:, 0, :], hv[:, 0:1], start=True, stop=False)
                    pe.matmul(ps_s[0:4, 100:101], k["mixs"][:, 1, :], hv[:, 1:2], start=False, stop=True).then_inc(s["p2"], 1)
                if piece == 2:
                    pe.wait_ge(s["sc4"], at(i, 1, 1))
                    pe.matmul(ps_s[:, 110:111], k["sel_w1"][:, :], sc4[:, :], start=True, stop=True).then_inc(s["p3"], 1)
                if piece == 3:
                    pe.wait_ge(s["hid"], at(i, 1, 1))
                    pe.matmul(ps_s[0:1, 120:124], hid[:, :], k["sel_w2"][:, :], start=True, stop=True).then_inc(s["p4"], 1)

            def mixer(i, p, nxt):
                for n in range(NT):
                    r = n_par(i, p, n)
                    pe.wait_ge(s["xh"], at(i, NT, n + 1))
                    wait(pe, s["t1"], i, NT, n)
                    wait(pe, s["t0"], i, NT, n)
                    for g in range(TG):
                        pe.transpose(ps_x[:, 0, g * GP:(g + 1) * GP], xh[:, r, g, 0:128], ident[0:GP, 0:GP])
                    for g in range(TG):
                        tr = pe.transpose(ps_x[0:C1, 1, g * GP:(g + 1) * GP], xh[:, r, g, 128:C], ident[0:GP, 0:GP])
                    tr.then_inc(s["turn"], 1)
                pe.wait_ge(s["t0"], at(i, NT, NT))
                pe.wait_ge(s["t1"], at(i, NT, NT))
                pe.wait_ge(s["perm"], at(i, 1, 1))
                alone(pe, s["pe_past"])
                by_column = pe.value_load(flag[0:1, p:p + 1], min_val=0, max_val=1)
                seqs = seq[:, :, :, :].rearrange("c v k s -> c (v k s)")
                base = pe.snap(by_column * (2 * XS))
                for n in range(NT + 1):
                    if n < NT:
                        for m in range(NB):
                            wait(pe, s["v"], i, NT * NB, NB * n + m - 2)
                            for c in range(2):
                                mm = pe.matmul(ps_f[:, m, 0:TP + 2], k["fc1"][:, c, m * 128:(m + 1) * 128],
                                               seqs[:, bass.ds(base + (c * XS + n * TP), TP + 2)], start=(c == 0), stop=(c == 1))
                            mm.then_inc(s["f1"], 1)
                    if n >= 1:
                        pe.wait_ge(s["g"], at(i, NT, n))
                        for q in range(2):
                            step = 2 * (n - 1) + q
                            if step < 2:
                                pe.wait_ge(s["x1"], at(i, HG, 2 * HG) if nxt is not None else B * HG)
                            wait(pe, s["o"], i, 2 * NT, step - 1)
                            for g in range(2):
                                for m in range(NB):
                                    a = (2 * q + g) * GP
                                    mm = pe.matmul(ps_o[0:GP, q, g * C:(g + 1) * C], gl[:, (n_par(i, p, n - 1)), m, a:a + GP],
                                                   k["fc2"][:, m, :], start=(m == 0), stop=(m == NB - 1))
                            mm.then_inc(s["f2"], 1)
                    if nxt is not None and n < 4:
                        select(nxt, 1 - p, n)

            schedule(pe, local, select, mixer)

        @block.scalar
        def _(act):
            def local(i, p):
                for n in range(CT):
                    act.wait_ge(s["conv"], at(i, CT, n + 1))
                    wait(act, s["xd"], i, CT, n - 1)
                    act.activation(tc[:, n % 2, :], ps_x[:, n % 2, 0:CP], ACT.Tanh, scale=0.4255).then_inc(s["th"], 1)

            def select(i, p, piece):
                if piece == 0:
                    act.wait_ge(s["p1"], at(i, 1, 1))
                    act.activation(absd[:, 0, 0:NG], ps_s[0:GP, 0:NG], ACT.Abs, accum_out=hv[:, 0:1])
                    act.activation(absd[:, 1, 0:2 * NG - 1], ps_s[0:GP, NG:3 * NG - 1], ACT.Abs, accum_out=hv[:, 1:2]).then_inc(s["hv"], 1)
                if piece == 1:
                    act.wait_ge(s["p2"], at(i, 1, 1))
                    act.activation(sc4[:, :], ps_s[0:4, 100:101], ACT.Abs).then_inc(s["sc4"], 1)
                if piece == 2:
                    act.wait_ge(s["p3"], at(i, 1, 1))
                    act.activation(hid[:, :], ps_s[:, 110:111], ACT.Relu, bias=k["sel_b1"][:, :]).then_inc(s["hid"], 1)

            def mixer(i, p, nxt):
                for n in range(NT):
                    act.wait_ge(s["turn"], at(i, NT, n + 1))
                    act.activation(seq[:, 0, 0, 1 + n * TP:1 + (n + 1) * TP], ps_x[:, 0, 0:TP], ACT.Copy).then_inc(s["t0"], 1)

                def middle(n):
                    r = n_par(i, p, n)
                    for m in range(NB):
                        act.wait_ge(s["f1"], at(i, NT * NB, NB * n + m + 1))
                        w1, b = k["dw"][:, m, 1:2], k["bias3"]
                        lo, hi = (1 if n == 0 else 0), (TP - 1 if n == NT - 1 else TP)
                        if n == 0:
                            act.activation(u[:, r, m, 0:1], ps_f[:, m, 1:2], ACT.Identity, scale=w1, bias=b[:, 1, m:m + 1])
                        if n == NT - 1:
                            act.activation(u[:, r, m, TP - 1:TP], ps_f[:, m, TP:TP + 1], ACT.Identity, scale=w1, bias=b[:, 2, m:m + 1])
                        act.activation(u[:, r, m, lo:hi], ps_f[:, m, 1 + lo:1 + hi], ACT.Identity, scale=w1,
                                       bias=b[:, 0, m:m + 1]).then_inc(s["u"], 1)

                def gelu(n):
                    r = n_par(i, p, n)
                    act.wait_ge(s["v"], at(i, NT * NB, NB * n + NB))
                    wait(act, s["f2"], i, 2 * NT, 2 * n - 2)
                    act.activation(gl[:, r, :, :], u[:, r, :, :], ACT.Gelu).then_inc(s["g"], 1)

                for n in range(NT + 1):
                    if n < NT:
                        if n >= 2:
                            act.wait_ge(s["g"], at(i, NT, n - 1))
                        else:
                            wait(act, s["g"], i, NT, n - 1)
                        middle(n)
                    if n >= 1:
                        gelu(n - 1)
                    if nxt is not None and n < 4:
                        select(nxt, 1 - p, n)

            schedule(act, local, select, mixer)

        @block.vector
        def _(dve):
            dve.memset(cw[0:D, :, 3:6, :], 0.0)
            dve.memset(seq[C1:128, :, 1, :], 0.0)
            dve.memset(seq[0:C1, :, 1, 0:XS:XS - 1], 0.0)
            dve.memset(seq[:, :, 0, 0:XS:XS - 1], 0.0).then_inc(s["zero"], 1)

            def local(i, p):
                for n in range(CT):
                    dve.wait_ge(s["th"], at(i, CT, n + 1))
                    if n == 0:
                        wait(dve, s["wu"], i, HG, 0)
                    dve.scalar_tensor_tensor(xd2[:, n * CP:(n + 1) * CP], tc[:, n % 2, :], 1.0, ps_x[:, n % 2, 0:CP],
                                             ALU.add, ALU.mult).then_inc(s["xd"], 1)

                def stats(g):
                    dve.wait_ge(s["x1"], at(i, HG, g + 1))
                    wait(dve, s["sg"], i, NG, 2 * g)
                    for a, c in enumerate((g, HG + g)):
                        dve.bn_stats(st[:, c, :], x1[:, p, c, :])
                        dve.tensor_tensor_reduce(junk[:, a, :], x1[:, p, c, :], k["gamma_r"][:, :], 1.0, 0.0, ALU.mult, ALU.add,
                                                 gs[:, c:c + 1]).then_inc(s["sg"], 1)

                dve.wait_ge(s["xb"], at(i, 1, 1))
                if not (isinstance(i, int) and i < 2):
                    dve.wait_ge(outs[p], (i - p) * (8 * NT))
                for g in range(HG):
                    dve.wait_ge(s["wu"], at(i, HG, g + 1))
                    dve.tensor_tensor(x1[:, p, g:NG:HG, :], ps_o[0:GP, g % 2, 0:2 * C].rearrange("p (a c) -> p a c", a=2),
                                      xin[:, g:NG:HG, :], ALU.add).then_inc(s["x1"], 1)
                    if g:
                        stats(g - 1)
                stats(HG - 1)
                dve.wait_ge(s["sg"], at(i, NG, NG))
                n0 = [0]

                def linked(op):
                    n0[0] += 1
                    op.then_inc(s["st"], 1)
                    dve.wait_ge(s["st"], at(i, 5, n0[0]))

                linked(dve.tensor_tensor(m_s[:, :], st[:, :, 1], st[:, :, 4], ALU.add))
                linked(dve.tensor_tensor(m_d[:, :], st[:, :, 1], st[:, :, 4], ALU.subtract))
                linked(dve.tensor_tensor(m_v[:, :], st[:, :, 2], st[:, :, 5], ALU.add))
                linked(dve.tensor_tensor(m_q[:, :], m_d[:, :], m_d[:, :], ALU.mult))
                linked(dve.tensor_scalar(m_v[:, :], m_v[:, :], 1.0 / C, EPS, ALU.mult, ALU.add))
                dve.scalar_tensor_tensor(var[:, :], m_q[:, :], 0.25, m_v[:, :], ALU.mult, ALU.add).then_inc(s["var"], 1)
                dve.wait_ge(s["rstd"], at(i, 1, 1))
                dve.scalar_tensor_tensor(nmr[:, p, :], m_s[:, :], -0.5, rstd[:, p, :], ALU.mult, ALU.mult).then_inc(s["nmr"], 1)
                dve.tensor_tensor(gr1[:, :], gs[:, :], rstd[:, p, :], ALU.mult).then_inc(s["gr1"], 1)
                dve.wait_ge(s["nmr"], at(i, 1, 1))
                dve.wait_ge(s["gr1"], at(i, 1, 1))
                wait(dve, s["p1"], i, 1, 0)
                dve.scalar_tensor_tensor(gray[:, :], nmr[:, p, :], k["gamma_sum"][:, :], gr1[:, :], ALU.mult, ALU.add).then_inc(s["gray"], 1)

            def select(i, p, piece):
                if piece != 3:
                    return
                dve.wait_ge(s["p4"], at(i, 1, 1))
                dve.tensor_tensor(lgt[:, :], ps_s[0:1, 120:124], k["sel_b2"][:, :], ALU.add).then_inc(s["l1"], 1)
                dve.wait_ge(s["l1"], at(i, 1, 1))
                dve.tensor_tensor(cmp[:, 0:1], lgt[:, 1:2], lgt[:, 0:1], ALU.is_gt)
                dve.tensor_tensor(cmp[:, 1:2], lgt[:, 1:2], lgt[:, 2:3], ALU.is_ge)
                dve.tensor_tensor(cmp[:, 2:3], lgt[:, 1:2], lgt[:, 3:4], ALU.is_ge).then_inc(s["l2"], 1)
                dve.wait_ge(s["l2"], at(i, 1, 1))
                dve.scalar_tensor_tensor(flag[:, p:p + 1], cmp[:, 0:1], cmp[:, 1:2], cmp[:, 2:3], ALU.mult, ALU.mult).then_inc(s["flag"], 1)

            def mixer(i, p, nxt):
                for n in range(NT):
                    dve.wait_ge(s["turn"], at(i, NT, n + 1))
                    dve.tensor_copy(seq[0:C1, 0, 1, 1 + n * TP:1 + (n + 1) * TP], ps_x[0:C1, 1, 0:TP]).then_inc(s["t1"], 1)

                def left(n, m):
                    r = n_par(i, p, n)
                    dve.wait_ge(s["u"], at(i, NT * NB, NB * n + m + 1))
                    dve.scalar_tensor_tensor(u[:, r, m, :], ps_f[:, m, 0:TP], k["dw"][:, m, 0:1], u[:, r, m, :],
                                             ALU.mult, ALU.add).then_inc(s["w"], 1)

                def right(n, m):
                    r = n_par(i, p, n)
                    dve.wait_ge(s["w"], at(i, NT * NB, NB * n + m + 1))
                    dve.scalar_tensor_tensor(u[:, r, m, :], ps_f[:, m, 2:TP + 2], k["dw"][:, m, 2:3], u[:, r, m, :],
                                             ALU.mult, ALU.add).then_inc(s["v"], 1)

                for n in range(NT + 1):
                    if n < NT:
                        left(n, 0)
                        left(n, 1)
                        right(n, 0)
                        left(n, 2)
                        right(n, 1)
                        right(n, 2)
                    if n >= 1:
                        if n == 1:
                            dve.wait_ge(s["x1b"], at(i, 1, 1))
                        for q in range(2):
                            step = 2 * (n - 1) + q
                            c = 2 * step
                            dve.wait_ge(s["f2"], at(i, 2 * NT, step + 1))
                            dve.tensor_tensor(x1[:, p, c:c + 2, :], ps_o[0:GP, q, 0:2 * C].rearrange("p (a c) -> p a c", a=2),
                                              x1[:, p, c:c + 2, :], ALU.add).then_inc(s["o"], 1)
                    if nxt is not None and n < 4:
                        select(nxt, 1 - p, n)

            schedule(dve, local, select, mixer)


def constants(np):
    diff = np.zeros((GP, 4, GP), np.float32)
    for m in range(GP):
        if m % W != W - 1:
            diff[m + 1, 0, m], diff[m, 0, m] = 1, -1
        if m < W:
            diff[m + W, 1, m], diff[m, 1, m] = 1, -1
        else:
            diff[m, 2, m] = -1
            diff[m - W, 3, m] = 1
    mixs = np.zeros((GP, 2, 4), np.float32)
    each = 1.0 / (C * H * (W - 1))
    mixs[:, 0, :] = [each, 0, 0.4 * each, each]
    mixs[:, 1, :] = [0, each, 0.4 * each, -each]
    return {"ident": np.eye(128, dtype=np.float32), "diff": diff, "mixs": mixs}


def kernel(**inputs):
    import numpy as np
    import concourse.bacc as bacc
    from concourse.bass_utils import run_bass_kernel_spmd

    a = {n: np.asarray(v) for n, v in inputs.items()}
    L0, L1 = "L0_conv_", "L1_conv_"
    col = lambda v: v.reshape(-1, 1)
    row = lambda v: v.reshape(1, -1)
    chan = lambda v: v.reshape(NB, 128).T
    laid = {
        "x": a["x"],
        "WdT0": a[L0 + "Wd"].T[0:128], "WdT1": a[L0 + "Wd"].T[128:], "W1T0": a[L0 + "W1"].T[0:128], "W1T1": a[L0 + "W1"].T[128:],
        "bd": col(a[L0 + "bd"]), "b1": col(a[L0 + "b1"]), "W2": a[L0 + "W2"], "W2T": a[L0 + "W2"].T, "b2": row(a[L0 + "b2"]),
        "tokT": a[L0 + "mask_token"].T, "WuT": a[L0 + "Wu"].T, "bu": row(a[L0 + "bu"]),
        "WhT": a[L0 + "Wh"].reshape(D, D, 9, D).transpose(3, 1, 2, 0).reshape(D, OC),
        "bh": a[L0 + "bh"].reshape(D, D, 9).transpose(1, 2, 0).reshape(1, OC),
        "fc1_0": a[L1 + "fc1_w"][0:128], "fc1_1": a[L1 + "fc1_w"][128:], "fc1_b": chan(a[L1 + "fc1_b"]),
        "gamma": row(a[L1 + "gamma"]), "gamma0": col(a[L1 + "gamma"])[0:128], "gamma1": col(a[L1 + "gamma"])[128:],
        "beta0": col(a[L1 + "beta"])[0:128], "beta1": col(a[L1 + "beta"])[128:],
        "dw_w": a[L1 + "dw_w"].reshape(NB, 128, 3).transpose(1, 0, 2), "dw_b": chan(a[L1 + "dw_b"]),
        "fc2_w": a[L1 + "fc2_w"].reshape(NB, 128, C).transpose(1, 0, 2), "fc2_b": row(a[L1 + "fc2_b"]),
        "sel_w1": a[L1 + "sel_w1"], "sel_b1": col(a[L1 + "sel_b1"]), "sel_w2": a[L1 + "sel_w2"], "sel_b2": row(a[L1 + "sel_b2"]),
        **constants(np),
    }
    nc = bacc.Bacc("TRN2", target_bir_lowering=False, num_devices=1)
    arrays, t = {}, {}
    for name, v in laid.items():
        arrays["in_" + name] = np.ascontiguousarray(v)
        t[name] = nc.dram_tensor("in_" + name, v.shape, F32, kind="ExternalInput").ap()
    out = nc.dram_tensor("out", (B, H, W, C), F32, kind="ExternalOutput").ap()
    t["map"] = nc.dram_tensor("map_scratch", (B, D, PADDED), F32, kind="Internal").ap()
    t["cw"] = nc.dram_tensor("cw_scratch", (B, OC), F32, kind="Internal").ap()
    t["cw_i"] = t["cw"].rearrange("b (c t d) -> b c t d", t=9, d=D)
    t["x_g"] = t["x"].rearrange("b (g r) w c -> b (r w) g c", r=2)
    t["out_g"] = out.rearrange("b (g r) w c -> b (r w) g c", r=2)
    build(nc, t)
    r = run_bass_kernel_spmd(nc, [arrays], core_ids=[0])
    return r.results[0]["out"]
```

```python
from contextlib import ExitStack

import concourse.bass as bass
from concourse import mybir

F32 = mybir.dt.float32
F32R = mybir.dt.float32r
I32 = mybir.dt.int32
ALU = mybir.AluOpType
ACT = mybir.ActivationFunctionType
AX = mybir.AxisListType

B, H, W, C = 32, 56, 56, 192
D = 64
M = 8
DI = 384
NB = DI // 128
SEL = 16
PIX = H * W
GP = 2 * W
NG = PIX // GP
TG = 4
NT = NG // TG
TP = TG * GP
C1 = C - 128
PW = W + 2
PADDED = PW * PW
CR = 7
CT = H // 2 // CR
CP = CR * W
HP = PIX // 2
HG = NG // 2
YW = M + D
TAPW = 9 * D
OC = D * TAPW
WCH = 9 * 512
NCH = OC // WCH
XS = PIX + 2
EPS = 1e-5


def build(nc, t):
    ctx = ExitStack()
    with ctx:
        def sem(name):
            return ctx.enter_context(nc.semaphore(name))

        def keep(name, shape, dt=F32):
            return ctx.enter_context(nc.sbuf_tensor(name, shape, dt))

        k = {}
        k["ident"] = keep("ident", [128, 128])
        k["w_ad"] = keep("w_ad", [128, 2, 128])
        k["bias_ad"] = keep("bias_ad", [128, 1])
        k["floor_ad"] = keep("floor_ad", [128, 1])
        k["pick"] = keep("pick", [128, YW])
        k["w2raw"] = keep("w2raw", [D, D])
        k["tokT"] = keep("tokT", [D, M])
        k["w2T"] = keep("w2T", [D + 1, D])
        k["ones"] = keep("ones", [M, 112])
        k["pooled"] = keep("pooled", [D + 1, B])
        k["mwf"] = keep("mwf", [D + 1, B])
        k["wu"] = keep("wu", [128, 2 * C])
        k["fc1"] = keep("fc1", [128, 2, DI])
        k["fc1_r"] = keep("fc1_r", [128, 4, DI], F32R)
        k["gamma_c"] = keep("gamma_c", [128, 2])
        k["beta_c"] = keep("beta_c", [128, 2])
        k["fc1_b"] = keep("fc1_b", [128, NB])
        k["dw"] = keep("dw", [128, NB, 3])
        k["dw_b"] = keep("dw_b", [128, NB])
        k["bias3"] = keep("bias3", [128, 3, NB])
        k["tmp3"] = keep("tmp3", [128, 2, NB])
        k["fc2"] = keep("fc2", [128, NB, C])
        k["gamma_r"] = keep("gamma_r", [GP, C])
        k["gamma_sum"] = keep("gamma_sum", [GP, 1])
        k["bu_r"] = keep("bu_r", [GP, C])
        k["fc2b_r"] = keep("fc2b_r", [GP, C])
        k["diff"] = keep("diff", [GP, 4, GP])
        k["mixs"] = keep("mixs", [GP, 2, 4])
        k["sel_w1"] = keep("sel_w1", [4, 128])
        k["sel_b1"] = keep("sel_b1", [128, 1])
        k["sel_w2"] = keep("sel_w2", [128, 4])
        k["sel_b2"] = keep("sel_b2", [1, 4])
        k["expo"] = keep("expo", [GP, NG])

        setup(nc, t, k, sem)
        pass_one(nc, t, k, sem)
        conv_weights(nc, t, k, sem)
        pass_two(nc, t, k, sem)


def at(i, per, n):
    return i * per + n


def wait(eng, s, i, per, n):
    v = i * per + n
    if isinstance(v, int) and v <= 0:
        return
    eng.wait_ge(s, v)


def alone(eng, s):
    eng.sem_inc(s, 1)


def setup(nc, t, k, sem):
    loads = [
        ("ident", k["ident"][:, :]), ("diff", k["diff"][:, :, :]), ("mixs", k["mixs"][:, :, :]),
        ("WdT0", k["w_ad"][:, 0, 0:D]), ("W1T0", k["w_ad"][:, 0, D:128]),
        ("WdT1", k["w_ad"][0:C1, 1, 0:D]), ("W1T1", k["w_ad"][0:C1, 1, D:128]),
        ("bd", k["bias_ad"][0:D, :]), ("b1", k["bias_ad"][D:128, :]),
        ("W2", k["w2raw"][:, :]), ("tokT", k["tokT"][:, :]),
        ("W2T", k["w2T"][0:D, :]), ("b2", k["w2T"][D:D + 1, :]),
        ("WuT", k["wu"][0:D, 0:C]), ("WuT", k["wu"][D:128, C:2 * C]),
        ("fc1_0", k["fc1"][:, 0, :]), ("fc1_1", k["fc1"][0:C1, 1, :]), ("fc1_1", k["fc1"][C1:128, 1, :]),
        ("gamma0", k["gamma_c"][:, 0:1]), ("gamma1", k["gamma_c"][0:C1, 1:2]),
        ("gamma1", k["gamma_c"][C1:128, 1:2]),
        ("beta0", k["beta_c"][:, 0:1]), ("beta1", k["beta_c"][0:C1, 1:2]),
        ("fc1_b", k["fc1_b"][:, :]), ("dw_w", k["dw"][:, :, :]), ("dw_b", k["dw_b"][:, :]),
        ("fc2_w", k["fc2"][:, :, :]),
        ("sel_w1", k["sel_w1"][:, 0:SEL]), ("sel_b1", k["sel_b1"][0:SEL, :]),
        ("sel_w2", k["sel_w2"][0:SEL, :]), ("sel_b2", k["sel_b2"][:, :]),
    ]
    rows = [("gamma", k["gamma_r"]), ("bu", k["bu_r"]), ("fc2_b", k["fc2b_r"])]
    weights_in, zeroed, small_mm, chain, parts = (sem(n) for n in ("weights_in", "zeroed", "small_mm", "chain", "parts"))
    total = 16 * (len(loads) + len(rows))
    with nc.psum_tensor("ps_tok", [128, M], F32) as ps_tok, \
            nc.psum_tensor("ps_beta", [128, NB, 1], F32) as ps_beta, nc.Block() as block:

        @block.sync
        def _(sp):
            sp.wait_ge(zeroed, 6)
            for name, dst in loads:
                sp.dma_start(dst, t[name]).then_inc(weights_in, 16)
            for name, dst in rows:
                sp.dma_start(dst[:, :], t[name].to_broadcast([GP, C])).then_inc(weights_in, 16)

        @block.vector
        def _(dve):
            dve.memset(k["w_ad"][:, 1, :], 0.0).then_inc(zeroed, 1)
            dve.memset(k["wu"][:, :], 0.0).then_inc(zeroed, 1)
            dve.memset(k["beta_c"][:, :], 0.0).then_inc(zeroed, 1)
            dve.memset(k["sel_w1"][:, :], 0.0).then_inc(zeroed, 1)
            dve.memset(k["sel_b1"][:, :], 0.0).then_inc(zeroed, 1)
            dve.memset(k["sel_w2"][:, :], 0.0).then_inc(zeroed, 1)
            dve.memset(k["pick"][0:D, :], 0.0)
            dve.memset(k["floor_ad"][0:D, :], -3.0e38)
            dve.memset(k["floor_ad"][D:128, :], 0.0)
            dve.memset(k["ones"][:, :], 1.0)
            dve.memset(k["mwf"][D:D + 1, :], 1.0)
            dve.memset(k["expo"][:, :], -0.5)
            dve.wait_ge(weights_in, total)
            dve.wait_ge(small_mm, 1)
            dve.tensor_copy(k["pick"][D:128, 0:M], ps_tok[D:128, :])
            dve.tensor_copy(k["pick"][D:128, M:YW], k["ident"][D:128, D:128])
            dve.tensor_scalar(k["wu"][:, :], k["wu"][:, :], 0.25, None, ALU.mult)
            for c in range(2):
                dve.tensor_scalar(k["fc1"][:, c, :], k["fc1"][:, c, :], k["gamma_c"][:, c:c + 1], None, ALU.mult).then_inc(parts, 1)
            dve.wait_ge(parts, 2)
            for c in range(2):
                dve.tensor_copy(k["fc1_r"][:, 2 * c, :], k["fc1"][:, c, :]).then_inc(parts, 1)
            dve.wait_ge(parts, 4)
            for c in range(2):
                dve.tensor_tensor(k["fc1_r"][:, 2 * c + 1, :], k["fc1"][:, c, :], k["fc1_r"][:, 2 * c, :].bitcast(F32), ALU.subtract)
            dve.reduce_sum(k["gamma_sum"][:, :], k["gamma_r"][:, :], AX.X)
            bp, ws = k["tmp3"][:, 0, :], k["tmp3"][:, 1, :]
            dve.tensor_tensor(bp, ps_beta[:, :, 0], k["fc1_b"][:, :], ALU.add)
            dve.tensor_tensor(ws, k["dw"][:, :, 0], k["dw"][:, :, 1], ALU.add).then_inc(chain, 1)
            dve.wait_ge(chain, 1)
            dve.tensor_tensor(ws, ws, k["dw"][:, :, 2], ALU.add).then_inc(chain, 1)
            dve.wait_ge(chain, 2)
            dve.tensor_tensor(ws, ws, bp, ALU.mult).then_inc(chain, 1)
            dve.wait_ge(chain, 3)
            dve.tensor_tensor(k["bias3"][:, 0, :], ws, k["dw_b"][:, :], ALU.add).then_inc(chain, 1)
            dve.wait_ge(chain, 4)
            dve.tensor_tensor(ws, k["dw"][:, :, 0], bp, ALU.mult).then_inc(chain, 1)
            dve.wait_ge(chain, 5)
            dve.tensor_tensor(k["bias3"][:, 1, :], k["bias3"][:, 0, :], ws, ALU.subtract).then_inc(chain, 1)
            dve.wait_ge(chain, 6)
            dve.tensor_tensor(ws, k["dw"][:, :, 2], bp, ALU.mult).then_inc(chain, 1)
            dve.wait_ge(chain, 7)
            dve.tensor_tensor(k["bias3"][:, 2, :], k["bias3"][:, 0, :], ws, ALU.subtract).then_inc(chain, 1)

        @block.tensor
        def _(pe):
            pe.wait_ge(weights_in, total)
            pe.matmul(ps_tok[D:128, :], k["w2raw"][:, :], k["tokT"][:, :], start=True, stop=True)
            for m in range(NB):
                for c in range(2):
                    mm = pe.matmul(ps_beta[:, m, :], k["fc1"][:, c, m * 128:(m + 1) * 128],
                                   k["beta_c"][:, c:c + 1], start=(c == 0), stop=(c == 1))
            mm.then_inc(small_mm, 1)


def pass_one(nc, t, k, sem):
    x_v, map_v = t["x_g"], t["map"]
    with ExitStack() as ctx:
        def sb(name, shape):
            return ctx.enter_context(nc.sbuf_tensor(name, shape, F32))

        def ps(name, shape):
            return ctx.enter_context(nc.psum_tensor(name, shape, F32))

        xa = sb("xa", [GP, 2, NG, C])
        xT = sb("xT", [128, 2, 2, TP])
        y = sb("y", [128, 2, TP])
        th = sb("th", [D, 2, TP])
        pad = sb("pad", [D, 2, PADDED])
        yl = sb("yl", [GP, 2, NG, YW + 1])
        mx = sb("mx", [GP, M])
        mx8 = sb("mx8", [M, 1])
        dg = sb("dg", [M, M])
        lg = sb("lg", [GP, NG, M])
        ex = sb("ex", [GP, NG, M])
        rz = sb("rz", [M, 1])
        pn = sb("pn", [M, D + 1])
        ps_c0 = ps("ps_c0", [128, 2, 512])
        ps_c1 = ps("ps_c1", [128, 1, 512])
        ps_a = ps("ps_a", [128, 2, 512])
        ps_y = ps("ps_y", [128, 2, 512])
        ps_q = ps("ps_q", [128, 512])
        x_in = [sem("x_in0"), sem("x_in1")]
        turned, c0_out, c1_out = sem("turned"), sem("c0_out"), sem("c1_out")
        proj, y_ready, th_ready, map_ready = sem("proj"), sem("y_ready"), sem("th_ready"), sem("map_ready")
        picked, yl_ready = sem("picked"), sem("yl_ready")
        map_out = [sem("map_out0"), sem("map_out1")]
        q_max, q_turn, q_m8, q_diag, q_bc, q_sub, q_exp = (sem("q_" + n) for n in ("max", "turn", "m8", "diag", "bc", "sub", "exp"))
        q_pool, q_rz, q_norm, q_sum, q_done = (sem("q_" + n) for n in ("pool", "rz", "norm", "sum", "done"))
        border = sem("border")
        block = ctx.enter_context(nc.Block())
        ident = k["ident"]

        def schedule(eng, features, pool):
            features(0, 0, None)
            features(1, 1, 0)
            with eng.Fori(2, B - 1, 2) as i:
                features(i, 0, 1)
                features(i + 1, 1, 0)
            for slot in range(NT):
                pool(B - 1, 1, slot)

        @block.sync
        def _(sp):
            sp.dma_start(xa[:, 0, :, :], x_v[0]).then_inc(x_in[0], 16)
            sp.dma_start(xa[:, 1, :, :], x_v[1]).then_inc(x_in[1], 16)

            def step(i, p, more):
                if more:
                    sp.wait_ge(turned, at(i, NT, NT))
                    sp.dma_start(xa[:, p, :, :], x_v[i + 2]).then_inc(x_in[p], 16)
                sp.wait_ge(map_ready, at(i, NT, NT))
                sp.dma_start(map_v[i], pad[:, p, :]).then_inc(map_out[p], 16)

            with sp.Fori(0, B - 3, 2) as i:
                step(i, 0, True)
                step(i + 1, 1, True)
            step(B - 2, 0, False)
            step(B - 1, 1, False)
            for p in range(2):
                sp.wait_ge(map_out[p], 16 * B // 2)

        @block.tensor
        def _(pe):
            def turn(i, p, n):
                if n == 0:
                    pe.wait_ge(x_in[p], (i - p) * 8 + 16)
                wait(pe, c1_out, i, NT, n)
                wait(pe, c0_out, i, NT, n - 1)
                for g in range(TG):
                    pe.transpose(ps_c0[:, n_par(i, p, n), g * GP:(g + 1) * GP], xa[:, p, n * TG + g, 0:128], ident[0:GP, 0:GP])
                for g in range(TG):
                    tr = pe.transpose(ps_c1[0:C1, 0, g * GP:(g + 1) * GP], xa[:, p, n * TG + g, 128:C], ident[0:GP, 0:GP])
                tr.then_inc(turned, 1)

            def project(i, p, n):
                r = n_par(i, p, n)
                pe.wait_ge(c0_out, at(i, NT, n + 1))
                pe.wait_ge(c1_out, at(i, NT, n + 1))
                wait(pe, y_ready, i, NT, n - 1)
                for c in range(2):
                    mm = pe.matmul(ps_a[:, r, 0:TP], k["w_ad"][:, c, :], xT[:, r, c, :], start=(c == 0), stop=(c == 1))
                mm.then_inc(proj, 1)

            def pick(i, p, n):
                r = n_par(i, p, n)
                pe.wait_ge(y_ready, at(i, NT, n + 1))
                wait(pe, yl_ready, i, NT, n - 1)
                for g in range(TG):
                    mm = pe.matmul(ps_y[0:GP, r, g * YW:(g + 1) * YW], y[:, r, g * GP:(g + 1) * GP], k["pick"][:, :], start=True, stop=True)
                mm.then_inc(picked, 1)

            def pool(i, p, slot):
                if slot == 0:
                    pe.wait_ge(q_max, at(i, 1, 1))
                    pe.transpose(ps_q[0:M, 0:GP], mx[:, :], ident[0:GP, 0:GP]).then_inc(q_turn, 1)
                if slot == 1:
                    pe.wait_ge(q_diag, at(i, 1, 1))
                    pe.matmul(ps_q[0:GP, 128:128 + M], k["ones"][:, :], dg[:, :], start=True, stop=True).then_inc(q_bc, 1)
                if slot == 3:
                    pe.wait_ge(q_exp, at(i, 1, 1))
                    for g in range(NG):
                        mm = pe.matmul(ps_q[0:M, 160:160 + D + 1], ex[:, g, :], yl[:, p, g, M:YW + 1], start=(g == 0), stop=(g == NG - 1))
                    mm.then_inc(q_pool, 1)
                if slot == 5:
                    pe.wait_ge(q_norm, at(i, 1, 1))
                    pe.matmul(ps_q[0:D + 1, 256:257], pn[:, :], k["ones"][:, 0:1], start=True, stop=True).then_inc(q_sum, 1)

            def features(i, p, q):
                for n in range(NT + 2):
                    if n < NT:
                        turn(i, p, n)
                    if 1 <= n <= NT:
                        project(i, p, n - 1)
                    if n >= 2:
                        pick(i, p, n - 2)
                        if q is not None:
                            pool(i - 1, q, n - 2)

            schedule(pe, features, pool)

        @block.scalar
        def _(act):
            def evac_c0(i, p, n):
                r = n_par(i, p, n)
                act.wait_ge(turned, at(i, NT, n + 1))
                wait(act, proj, i, NT, n - 1)
                act.activation(xT[:, r, 0, :], ps_c0[:, r, 0:TP], ACT.Copy).then_inc(c0_out, 1)

            def tanh(i, p, n):
                r = n_par(i, p, n)
                act.wait_ge(y_ready, at(i, NT, n + 1))
                wait(act, map_ready, i, NT, n - 1)
                act.activation(th[:, r, :], y[0:D, r, :], ACT.Tanh, scale=0.851).then_inc(th_ready, 1)

            def evac_y(i, p, n):
                r = n_par(i, p, n)
                act.wait_ge(picked, at(i, NT, n + 1))
                if n == 0:
                    wait(act, q_pool, i, 1, -1)
                act.activation(yl[:, p, n * TG:(n + 1) * TG, 0:YW],
                               ps_y[0:GP, r, 0:TG * YW].rearrange("p (g w) -> p g w", w=YW), ACT.Copy).then_inc(yl_ready, 1)

            def pool(i, p, slot):
                if slot == 2:
                    act.wait_ge(q_sub, at(i, 1, 1))
                    wait(act, q_pool, i, 1, 0)
                    act.activation(ex[:, :, :], lg[:, :, :], ACT.Exp).then_inc(q_exp, 1)

            def features(i, p, q):
                for n in range(NT + 2):
                    if n < NT:
                        evac_c0(i, p, n)
                    if 1 <= n <= NT:
                        tanh(i, p, n - 1)
                    if n >= 2:
                        evac_y(i, p, n - 2)
                        if q is not None:
                            pool(i - 1, q, n - 2)

            schedule(act, features, pool)

        @block.vector
        def _(dve):
            dve.memset(xT[64:128, :, 1, :], 0.0).then_inc(border, 1)
            dve.memset(pad[:, :, :], 0.0).then_inc(border, 1)
            dve.memset(yl[:, :, :, YW:YW + 1], 1.0).then_inc(border, 1)
            dve.wait_ge(border, 3)

            def evac_c1(i, p, n):
                r = n_par(i, p, n)
                dve.wait_ge(turned, at(i, NT, n + 1))
                wait(dve, proj, i, NT, n - 1)
                dve.tensor_copy(xT[0:C1, r, 1, :], ps_c1[0:C1, 0, 0:TP]).then_inc(c1_out, 1)

            def biased(i, p, n):
                r = n_par(i, p, n)
                dve.wait_ge(proj, at(i, NT, n + 1))
                wait(dve, picked, i, NT, n - 1)
                wait(dve, th_ready, i, NT, n - 1)
                wait(dve, map_ready, i, NT, n - 1)
                dve.tensor_scalar(y[:, r, :], ps_a[:, r, 0:TP], k["bias_ad"][:, :], k["floor_ad"][:, :],
                                  ALU.add, ALU.max).then_inc(y_ready, 1)

            def gelu_map(i, p, n):
                r = n_par(i, p, n)
                dve.wait_ge(th_ready, at(i, NT, n + 1))
                if n == 0 and not (isinstance(i, int) and i < 2):
                    dve.wait_ge(map_out[p], (i - p) * 8)
                rows = pad[:, p, PW + n * (TP // W) * PW:PW + (n + 1) * (TP // W) * PW].rearrange("c (h w) -> c h w", w=PW)
                dve.scalar_tensor_tensor(rows[:, :, 1:W + 1], th[:, r, :].rearrange("c (h w) -> c h w", w=W), 1.0,
                                         y[0:D, r, :].rearrange("c (h w) -> c h w", w=W), ALU.add, ALU.mult).then_inc(map_ready, 1)

            def pool(i, p, slot):
                if slot == 0:
                    dve.wait_ge(yl_ready, at(i, NT, NT))
                    wait(dve, q_turn, i, 1, 0)
                    dve.tensor_reduce(mx[:, :], yl[:, p, :, 0:M].rearrange("p g m -> p m g"), AX.X, ALU.max).then_inc(q_max, 1)
                    dve.wait_ge(q_turn, at(i, 1, 1))
                    dve.tensor_reduce(mx8[:, :], ps_q[0:M, 0:GP], AX.X, ALU.max).then_inc(q_m8, 1)
                    dve.wait_ge(q_m8, at(i, 1, 1))
                    dve.tensor_scalar(dg[:, :], ident[0:M, 0:M], mx8[:, :], None, ALU.mult).then_inc(q_diag, 1)
                if slot == 1:
                    dve.wait_ge(q_bc, at(i, 1, 1))
                    dve.tensor_tensor(lg[:, :, :].rearrange("p g m -> p m g"), yl[:, p, :, 0:M].rearrange("p g m -> p m g"),
                                      ps_q[0:GP, 128:128 + M].unsqueeze(2).to_broadcast([GP, M, NG]), ALU.subtract).then_inc(q_sub, 1)
                if slot == 4:
                    dve.wait_ge(q_pool, at(i, 1, 1))
                    dve.reciprocal(rz[:, :], ps_q[0:M, 160 + D:161 + D]).then_inc(q_rz, 1)
                    dve.wait_ge(q_rz, at(i, 1, 1))
                    dve.tensor_scalar(pn[:, :], ps_q[0:M, 160:161 + D], rz[:, :], None, ALU.mult).then_inc(q_norm, 1)
                if slot == 6:
                    dve.wait_ge(q_sum, at(i, 1, 1))
                    dve.tensor_copy(k["pooled"][:, bass.ds(i, 1)], ps_q[0:D + 1, 256:257]).then_inc(q_done, 1)

            def features(i, p, q):
                for n in range(NT + 2):
                    if n < NT:
                        evac_c1(i, p, n)
                    if 1 <= n <= NT:
                        biased(i, p, n - 1)
                    if n >= 2:
                        gelu_map(i, p, n - 2)
                        if q is not None:
                            pool(i - 1, q, n - 2)

            schedule(dve, features, pool)


def n_par(i, p, n):
    return (p * NT + n) % 2


def conv_weights(nc, t, k, sem):
    with ExitStack() as ctx:
        wh = ctx.enter_context(nc.sbuf_tensor("wh", [D + 1, 2, WCH], F32))
        cwo = ctx.enter_context(nc.sbuf_tensor("cwo", [B, 2, WCH], F32))
        ps_m = ctx.enter_context(nc.psum_tensor("ps_m", [128, 512], F32))
        ps_h = ctx.enter_context(nc.psum_tensor("ps_h", [128, 4, 512], F32))
        wh_in = [sem("wh_in0"), sem("wh_in1")]
        mwf_mm, mwf_ready, hyper, hyper_out = (sem(n) for n in ("mwf_mm", "mwf_ready", "hyper", "hyper_out"))
        cw_out = [sem("cw_out0"), sem("cw_out1")]
        N = WCH // 512
        block = ctx.enter_context(nc.Block())

        @block.sync
        def _(sp):
            for j in range(NCH + 2):
                if j < NCH:
                    if j >= 2:
                        sp.wait_ge(hyper, N * (j - 1))
                    sp.dma_start(wh[0:D, j % 2, :], t["WhT"][:, j * WCH:(j + 1) * WCH]).then_inc(wh_in[j % 2], 16)
                    sp.dma_start(wh[D:D + 1, j % 2, :], t["bh"][:, j * WCH:(j + 1) * WCH]).then_inc(wh_in[j % 2], 16)
                if j >= 2:
                    sp.wait_ge(hyper_out, N * (j - 1))
                    sp.dma_start(t["cw"][:, (j - 2) * WCH:(j - 1) * WCH], cwo[:, j % 2, :]).then_inc(cw_out[j % 2], 16)
            for r in range(2):
                sp.wait_ge(cw_out[r], 16 * NCH // 2)

        @block.tensor
        def _(pe):
            pe.matmul(ps_m[0:D, 0:B], k["w2T"][:, :], k["pooled"][:, :], start=True, stop=True).then_inc(mwf_mm, 1)
            pe.wait_ge(mwf_ready, 1)
            for j in range(NCH):
                pe.wait_ge(wh_in[j % 2], 32 * (j // 2 + 1))
                for n in range(N):
                    s = j * N + n
                    if s >= 4:
                        pe.wait_ge(hyper_out, s - 3)
                    pe.matmul(ps_h[0:B, s % 4, :], k["mwf"][:, :], wh[:, j % 2, n * 512:(n + 1) * 512],
                              start=True, stop=True).then_inc(hyper, 1)

        @block.vector
        def _(dve):
            dve.wait_ge(mwf_mm, 1)
            dve.tensor_copy(k["mwf"][0:D, :], ps_m[0:D, 0:B]).then_inc(mwf_ready, 1)
            for j in range(NCH):
                if j >= 2:
                    dve.wait_ge(cw_out[j % 2], 16 * (j // 2))
                for n in range(N):
                    s = j * N + n
                    dve.wait_ge(hyper, s + 1)
                    dve.tensor_copy(cwo[:, j % 2, n * 512:(n + 1) * 512], ps_h[0:B, s % 4, :]).then_inc(hyper_out, 1)


PLAN = {
    (0, "A"): [("conv", 0)], (0, "B"): [("wu", 0), ("wu", 1)], (0, "C"): [("conv", 1)],
    (1, "A"): [("wu", 2), ("wu", 3)], (1, "B"): [("conv", 2)], (1, "C"): [("wu", 4), ("wu", 5)],
    (2, "A"): [("wu", 6), ("wu", 7)], (2, "B"): [("conv", 3)], (2, "C"): [("wu", 8), ("wu", 9)],
    (3, "A"): [("wu", 10), ("wu", 11)], (3, "B"): [("wu", 12)], (3, "C"): [("wu", 13), ("norm", 0)],
    (4, "C"): [("split", 0)],
    (5, "A"): [("select", 0), ("split", 1), ("turn", 0)], (5, "B"): [("select", 1), ("split", 2), ("turn", 1)],
    (5, "C"): [("select", 2), ("split", 3), ("turn", 2)],
    (6, "A"): [("select", 3), ("split", 4), ("turn", 3)], (6, "B"): [("split", 5), ("turn", 4)],
    (6, "C"): [("split", 6), ("turn", 5)],
    (7, "A"): [("turn", 6)],
}
SLOTS = NT + 1
T_ACT, T_DVE = 11, 10


def pass_two(nc, t, k, sem):
    x_v, map_v, cw_v, out_v = t["x_g"], t["map"], t["cw_i"], t["out_g"]
    with ExitStack() as ctx:
        def sb(name, shape, dt=F32):
            return ctx.enter_context(nc.sbuf_tensor(name, shape, dt))

        def ps(name, shape):
            return ctx.enter_context(nc.psum_tensor(name, shape, F32))

        x1 = sb("x1", [GP, 2, NG, C])
        pads = sb("pads", [128, PADDED])
        cw = sb("cw_s", [128, 6, D])
        tc = sb("tc", [128, 2, CP])
        xd2 = sb("xd2", [128, HP])
        st = sb("st", [GP, NG, 6])
        gs = sb("gs", [GP, NG])
        junk = sb("junk", [GP, 2, C])
        m_s, m_d, m_v, m_q, var = (sb(n, [GP, NG]) for n in ("m_s", "m_d", "m_v", "m_q", "var"))
        rstd = sb("rstd", [GP, NG])
        nmr = sb("nmr", [GP, NG])
        gr1 = sb("gr1", [GP, NG])
        gray = sb("gray", [GP, NG])
        absd = sb("absd", [GP, 2, 2 * NG])
        hv = sb("hv", [GP, 2])
        sc4 = sb("sc4", [4, 1])
        hid = sb("hid", [128, 1])
        lgt = sb("lgt", [1, 4])
        cmp = sb("cmp", [1, 4])
        flag = sb("flag", [1, 1], I32)
        xh = sb("xh", [GP, 2, TG, C])
        xs = sb("xs", [GP, 2, TG, 2 * C])
        seq = sb("seq", [128, 2, 3, XS], F32R)
        ug = sb("ug", [128, 2, 2, NB, TP])
        u, gl = ug[:, 0], ug[:, 1]
        spare = ug[:, :, :, :, :].rearrange("c a b m s -> c (a b m s)")[:, 0:PIX]
        ps_x = ps("ps_x", [128, 2, 512])
        ps_w0 = ps("ps_w0", [128, 512])
        ps_w1 = ps("ps_w1", [128, 512])
        ps_o = ps("ps_o", [128, 512])
        ps_f = ps("ps_f", [128, NB, 512])
        ps_w, ps_s = [ps_w0, ps_w1], ps_w1
        s = {n: sem("t_" + n) for n in (
            "xb", "conv", "th", "xd", "wu", "x1", "sg", "st", "var", "rstd", "nmr", "gr1", "gray",
            "p1", "hv", "p2", "sc4", "p3", "hid", "p4", "l1", "l2", "flag", "xh", "hi", "lo", "x1b", "turn", "t0", "t1",
            "perm", "f1", "u", "w", "v", "g", "f2", "o", "zero", "vcopy", "pool_past")}
        cin = sem("cin")
        x_in = [sem("x2_in0"), sem("x2_in1")]
        outs = [sem("outs0"), sem("outs1")]
        block = ctx.enter_context(nc.Block())
        ident = k["ident"]
        MX = NT * NB

        def schedule(eng, slot, item):
            def items(i, p, n, place):
                for what, j in PLAN.get((n, place), []):
                    item[what](i, p, j)

            def turn_of(i, p, ahead):
                for n in range(SLOTS):
                    slot(i, p, n, ahead is not None, lambda place, n=n: items(ahead, 1 - p, n, place) if ahead is not None else None)

            for n in range(SLOTS):
                for place in "ABC":
                    items(0, 0, n, place)
            turn_of(0, 0, 1)
            with eng.Fori(1, B - 2, 2) as i:
                turn_of(i, 1, i + 1)
                turn_of(i + 1, 0, i + 2)
            turn_of(B - 1, 1, None)

        def nothing(i, p, j):
            pass

        def pairs(ap, j):
            return ap.rearrange("p (a g) c -> p a g c", a=2)[:, :, 2 * j:2 * j + 2, :]

        def halves(ap, h):
            return ap.rearrange("p (a g) c -> p a g c", a=2)[:, :, h * 7:h * 7 + 7, :]

        @block.sync
        def _(sp):
            def load_conv(i):
                sp.dma_start(pads[0:D, :], map_v[i]).then_inc(cin, 16)
                sp.dma_start(pads[D:128, 0:PADDED - PW], map_v[i][:, PW:PADDED]).then_inc(cin, 16)
                sp.dma_start(cw[0:D, 0:3, :], cw_v[i][:, 0:3, :]).then_inc(cin, 16)
                sp.dma_start(cw[D:128, :, :], cw_v[i][:, 3:9, :]).then_inc(cin, 16)

            def load_x(i, p, h):
                for a in range(2):
                    g = a * HG + h * 7
                    sp.dma_start(x1[:, p, g:g + 7, :], x_v[i][:, g:g + 7, :]).then_inc(x_in[h], 16)

            def turn_of(i, p, conv_next, x_next):
                for n in range(NT):
                    if n == 3 and conv_next:
                        sp.wait_ge(s["conv"], at(i, CT, 2 * CT))
                        load_conv(i + 2)
                    if n == NT - 1 and x_next:
                        sp.wait_ge(outs[p], (i - p) * (8 * NT) + 16 * (NT - 1))
                        load_x(i + 2, p, 0)
                    sp.wait_ge(s["o"], at(i, 2 * NT, 2 * n + 2))
                    sp.dma_start(out_v[i][:, n * TG:(n + 1) * TG, :], x1[:, p, n * TG:(n + 1) * TG, :]).then_inc(outs[p], 16)
                if x_next:
                    sp.wait_ge(outs[p], (i - p) * (8 * NT) + 16 * NT)
                    load_x(i + 2, p, 1)

            sp.wait_ge(s["zero"], 1)
            for h in range(2):
                load_x(0, 0, h)
            load_conv(0)
            for h in range(2):
                sp.wait_ge(x_in[h], 32)
                load_x(1, 1, h)
            sp.wait_ge(s["conv"], CT)
            load_conv(1)
            turn_of(0, 0, True, True)
            with sp.Fori(1, B - 4, 2) as i:
                turn_of(i, 1, True, True)
                turn_of(i + 1, 0, True, True)
            turn_of(B - 3, 1, True, True)
            turn_of(B - 2, 0, False, False)
            turn_of(B - 1, 1, False, False)
            for p in range(2):
                sp.wait_ge(outs[p], 16 * NT * B // 2)

        @block.gpsimd
        def _(pool):
            def add_bu(i, p, h):
                pool.wait_ge(x_in[h], at(i, 32, 32))
                alone(pool, s["pool_past"])
                for a in range(2):
                    g = a * HG + h * 7
                    op = pool.tensor_tensor(x1[:, p, g:g + 7, :], x1[:, p, g:g + 7, :],
                                            k["bu_r"][:, :].unsqueeze(1).to_broadcast([GP, 7, C]), ALU.add)
                op.then_inc(s["xb"], 1)

            def normalise(i, p):
                pool.wait_ge(s["var"], at(i, 1, 1))
                wait(pool, s["gray"], i, 1, 0)
                wait(pool, s["xh"], i, NT, 0)
                pool.tensor_tensor(rstd[:, :], var[:, :], k["expo"][:, :], ALU.pow).then_inc(s["rstd"], 1)
                pool.wait_ge(s["nmr"], at(i, 1, 1))
                pool.wait_ge(s["rstd"], at(i, 1, 1))
                for j in range(NT):
                    r = n_par(i, p, j)
                    wait(pool, s["lo"], i, NT, j - 1)
                    alone(pool, s["pool_past"])
                    for g in range(TG):
                        c = (g // 2) * HG + 2 * j + g % 2
                        op = pool.tensor_scalar(xh[:, r, g, :], x1[:, p, c, :], rstd[:, c:c + 1], nmr[:, c:c + 1],
                                                ALU.mult, ALU.add)
                    op.then_inc(s["xh"], 1)

            def column_order(i, p):
                pool.wait_ge(s["t0"], at(i, T_ACT, T_ACT))
                pool.wait_ge(s["t1"], at(i, T_DVE, T_DVE))
                pool.wait_ge(s["flag"], at(i, 1, 1))
                alone(pool, s["pool_past"])
                by_column = pool.value_load(flag[0:1, 0:1], min_val=0, max_val=1)
                with pool.If(by_column):
                    wait(pool, s["f2"], i, 2 * NT, 0)
                    for c in range(3):
                        if c:
                            pool.wait_ge(s["vcopy"], at(i, 6, 2 * c))
                        alone(pool, s["pool_past"])
                        rows = seq[:, p, c, 1:1 + PIX]
                        pool.tensor_copy(spare.rearrange("c (w h) -> c w h", h=H),
                                         rows.bitcast(F32).rearrange("c (h w) -> c w h", w=W)).then_inc(s["vcopy"], 1)
                        pool.wait_ge(s["vcopy"], at(i, 6, 2 * c + 1))
                        alone(pool, s["pool_past"])
                        pool.tensor_copy(rows, spare).then_inc(s["vcopy"], 1)
                with pool.Else():
                    pool.sem_inc(s["vcopy"], 6)
                pool.wait_ge(s["vcopy"], at(i, 6, 6))
                pool.sem_inc(s["perm"], 1)

            def add_fc2b(i, p, tiles):
                if tiles[0] == 0:
                    pool.wait_ge(s["xh"], at(i, NT, NT))
                    pool.wait_ge(s["perm"], at(i, 1, 1))
                for n in tiles:
                    c = n * TG
                    pool.tensor_tensor(x1[:, p, c:c + TG, :], x1[:, p, c:c + TG, :],
                                       k["fc2b_r"][:, :].unsqueeze(1).to_broadcast([GP, TG, C]), ALU.add).then_inc(s["x1b"], 1)

            def turn_of(i, p, ahead):
                if ahead is not None:
                    add_bu(ahead, 1 - p, 0)
                add_fc2b(i, p, range(0, 2))
                if ahead is not None:
                    add_bu(ahead, 1 - p, 1)
                add_fc2b(i, p, range(2, NT))
                if ahead is not None:
                    normalise(ahead, 1 - p)
                    column_order(ahead, 1 - p)

            for h in range(2):
                add_bu(0, 0, h)
            normalise(0, 0)
            column_order(0, 0)
            turn_of(0, 0, 1)
            with pool.Fori(1, B - 2, 2) as i:
                turn_of(i, 1, i + 1)
                turn_of(i + 1, 0, i + 2)
            turn_of(B - 1, 1, None)

        @block.tensor
        def _(pe):
            def conv(i, p, n):
                if n == 0:
                    pe.wait_ge(cin, at(i, 64, 64))
                    wait(pe, s["t0"], i, T_ACT, 0)
                    wait(pe, s["t1"], i, T_DVE, 0)
                wait(pe, s["xd"], i, CT, n - 1)
                for tap in range(6):
                    down = tap // 3
                    for half in range(2):
                        o = (half * H // 2 + n * CR + down) * PW
                        mv = pads[:, o:o + CR * PW].rearrange("c (h w) -> c h w", w=PW)[:, :, tap % 3:tap % 3 + W]
                        mm = pe.matmul(ps_x[half * D:(half + 1) * D, n % 2, 0:CP], cw[:, tap, :], mv,
                                       start=(tap == 0), stop=(tap == 5))
                mm.then_inc(s["conv"], 1)

            def wu(i, p, g):
                pe.wait_ge(s["xd"], at(i, CT, (g * GP + GP - 1) // CP + 1))
                if g == 0:
                    wait(pe, s["flag"], i, 1, 0)
                wait(pe, s["x1"], i, HG, g - 1)
                pe.matmul(ps_w[g % 2][0:GP, 0:2 * C], xd2[:, g * GP:(g + 1) * GP], k["wu"][:, :],
                          start=True, stop=True).then_inc(s["wu"], 1)

            def select(i, p, piece):
                if piece == 0:
                    pe.wait_ge(s["gray"], at(i, 1, 1))
                    pe.wait_ge(s["x1"], at(i, HG, HG))
                    pe.matmul(ps_s[0:GP, 0:NG], k["diff"][:, 0, :], gray[:, :], start=True, stop=True)
                    pe.matmul(ps_s[0:GP, NG:2 * NG], k["diff"][:, 1, :], gray[:, :], start=True, stop=True)
                    pe.matmul(ps_s[0:GP, 2 * NG:3 * NG - 1], k["diff"][:, 2, :], gray[:, 0:NG - 1], start=True, stop=False)
                    pe.matmul(ps_s[0:GP, 2 * NG:3 * NG - 1], k["diff"][:, 3, :], gray[:, 1:NG], start=False, stop=True).then_inc(s["p1"], 1)
                if piece == 1:
                    pe.wait_ge(s["hv"], at(i, 1, 1))
                    pe.matmul(ps_s[0:4, 100:101], k["mixs"][:, 0, :], hv[:, 0:1], start=True, stop=False)
                    pe.matmul(ps_s[0:4, 100:101], k["mixs"][:, 1, :], hv[:, 1:2], start=False, stop=True).then_inc(s["p2"], 1)
                if piece == 2:
                    pe.wait_ge(s["sc4"], at(i, 1, 1))
                    pe.matmul(ps_s[:, 110:111], k["sel_w1"][:, :], sc4[:, :], start=True, stop=True).then_inc(s["p3"], 1)
                if piece == 3:
                    pe.wait_ge(s["hid"], at(i, 1, 1))
                    pe.matmul(ps_s[0:1, 120:124], hid[:, :], k["sel_w2"][:, :], start=True, stop=True).then_inc(s["p4"], 1)

            def turn(i, p, j):
                r = n_par(i, p, j)
                pe.wait_ge(s["hi"], at(i, NT, j + 1))
                pe.wait_ge(s["lo"], at(i, NT, j + 1))
                for c in range(3):
                    n = 3 * j + c
                    if n % 2 == 0:
                        wait(pe, s["t0"], i, T_ACT, n // 2)
                    else:
                        wait(pe, s["t1"], i, T_DVE, n // 2)
                    for g in range(TG):
                        src = xs[:, r, g, (0, 2 * 128, 128)[c]:][:, 0:128]
                        tr = pe.transpose(ps_x[:, n % 2, g * GP:(g + 1) * GP], src, ident[0:GP, 0:GP])
                    tr.then_inc(s["turn"], 1)

            def fc1(i, p, n, m):
                if n == 0 and m == 0:
                    pe.wait_ge(s["perm"], at(i, 1, 1))
                wait(pe, s["v"], i, MX, NB * n + m - 2)
                cols = slice(m * 128, (m + 1) * 128)
                at_ = slice(n * TP, n * TP + TP + 2)
                parts = ((0, 0), (0, 1), (1, 0), (2, 2), (3, 2))
                for q, (w, c) in enumerate(parts):
                    mm = pe.matmul(ps_f[:, m, 0:TP + 2], k["fc1_r"][:, w, cols], seq[:, p, c, at_],
                                   start=(q == 0), stop=(q == len(parts) - 1))
                mm.then_inc(s["f1"], 1)

            def fc2(i, p, n, q):
                r = n_par(i, p, n)
                pe.wait_ge(s["g"], at(i, NT, n + 1))
                wait(pe, s["o"], i, 2 * NT, 2 * n + q)
                for g in range(2):
                    for m in range(NB):
                        a = (2 * q + g) * GP
                        mm = pe.matmul(ps_o[0:GP, g * C:(g + 1) * C], gl[:, r, m, a:a + GP], k["fc2"][:, m, :],
                                       start=(m == 0), stop=(m == NB - 1))
                mm.then_inc(s["f2"], 1)

            def slot(i, p, n, ahead, place):
                if n < NT:
                    fc1(i, p, n, 0)
                place("A")
                if n < NT:
                    fc1(i, p, n, 1)
                if n:
                    fc2(i, p, n - 1, 0)
                place("B")
                if n < NT:
                    fc1(i, p, n, 2)
                if n:
                    fc2(i, p, n - 1, 1)
                place("C")

            schedule(pe, slot, {"conv": conv, "wu": wu, "norm": nothing, "split": nothing, "turn": turn, "select": select})

        def unit_of(ap, j):
            return ap.rearrange("c (a s) -> c a s", a=2)[:, :, 2 * j * GP:2 * (j + 1) * GP]

        @block.scalar
        def _(act):
            def conv(i, p, n):
                act.wait_ge(s["conv"], at(i, CT, n + 1))
                wait(act, s["xd"], i, CT, n - 1)
                act.activation(tc[:, n % 2, :], ps_x[:, n % 2, 0:CP], ACT.Tanh, scale=0.4255).then_inc(s["th"], 1)

            def select(i, p, piece):
                if piece == 0:
                    act.wait_ge(s["p1"], at(i, 1, 1))
                    act.activation(absd[:, 0, 0:NG], ps_s[0:GP, 0:NG], ACT.Abs, accum_out=hv[:, 0:1])
                    act.activation(absd[:, 1, 0:2 * NG - 1], ps_s[0:GP, NG:3 * NG - 1], ACT.Abs, accum_out=hv[:, 1:2]).then_inc(s["hv"], 1)
                if piece == 1:
                    act.wait_ge(s["p2"], at(i, 1, 1))
                    act.activation(sc4[:, :], ps_s[0:4, 100:101], ACT.Abs).then_inc(s["sc4"], 1)
                if piece == 2:
                    act.wait_ge(s["p3"], at(i, 1, 1))
                    act.activation(hid[:, :], ps_s[:, 110:111], ACT.Relu, bias=k["sel_b1"][:, :]).then_inc(s["hid"], 1)

            def split(i, p, j):
                r = n_par(i, p, j)
                act.wait_ge(s["xh"], at(i, NT, j + 1))
                wait(act, s["turn"], i, 3 * NT, 3 * (j - 1))
                act.activation(xs[:, r, :, 0:C].bitcast(F32R), xh[:, r, :, :], ACT.Copy).then_inc(s["hi"], 1)

            def turn(i, p, j):
                for n in range(3 * j, 3 * j + 3):
                    if n % 2 == 0:
                        act.wait_ge(s["turn"], at(i, 3 * NT, n + 1))
                        act.activation(unit_of(seq[:, p, n % 3, 1:1 + PIX], j), ps_x[:, 0, 0:TP].rearrange("c (a s) -> c a s", a=2),
                                       ACT.Copy).then_inc(s["t0"], 1)

            def middle(i, p, n, m):
                r = n_par(i, p, n)
                act.wait_ge(s["f1"], at(i, MX, NB * n + m + 1))
                w1, b = k["dw"][:, m, 1:2], k["bias3"]
                lo, hi = (1 if n == 0 else 0), (TP - 1 if n == NT - 1 else TP)
                if n == 0:
                    act.activation(u[:, r, m, 0:1], ps_f[:, m, 1:2], ACT.Identity, scale=w1, bias=b[:, 1, m:m + 1])
                if n == NT - 1:
                    act.activation(u[:, r, m, TP - 1:TP], ps_f[:, m, TP:TP + 1], ACT.Identity, scale=w1, bias=b[:, 2, m:m + 1])
                act.activation(u[:, r, m, lo:hi], ps_f[:, m, 1 + lo:1 + hi], ACT.Identity, scale=w1,
                               bias=b[:, 0, m:m + 1]).then_inc(s["u"], 1)

            def gelu(i, p, n):
                r = n_par(i, p, n)
                act.wait_ge(s["v"], at(i, MX, NB * n + NB))
                wait(act, s["f2"], i, 2 * NT, 2 * n - 2)
                act.activation(gl[:, r, :, :], u[:, r, :, :], ACT.Gelu).then_inc(s["g"], 1)

            def slot(i, p, n, ahead, place):
                if n:
                    gelu(i, p, n - 1)
                if n < NT:
                    wait(act, s["g"], i, NT, n - 1)
                    middle(i, p, n, 0)
                place("A")
                if n < NT:
                    middle(i, p, n, 1)
                place("B")
                if n < NT:
                    middle(i, p, n, 2)
                place("C")

            schedule(act, slot, {"conv": conv, "wu": nothing, "norm": nothing, "split": split, "turn": turn, "select": select})

        @block.vector
        def _(dve):
            dve.memset(cw[0:D, 3:6, :], 0.0)
            dve.memset(seq[:, :, :, 0:XS:XS - 1].bitcast(F32), 0.0).then_inc(s["zero"], 1)

            def conv(i, p, n):
                dve.wait_ge(s["th"], at(i, CT, n + 1))
                if n == 0:
                    wait(dve, s["wu"], i, HG, 0)
                dve.scalar_tensor_tensor(xd2[:, n * CP:(n + 1) * CP], tc[:, n % 2, :], 1.0, ps_x[:, n % 2, 0:CP],
                                         ALU.add, ALU.mult).then_inc(s["xd"], 1)

            def stats(i, p, g):
                dve.wait_ge(s["x1"], at(i, HG, g + 1))
                wait(dve, s["sg"], i, NG, 2 * g)
                for a, c in enumerate((g, HG + g)):
                    dve.bn_stats(st[:, c, :], x1[:, p, c, :])
                    dve.tensor_tensor_reduce(junk[:, a, :], x1[:, p, c, :], k["gamma_r"][:, :], 1.0, 0.0, ALU.mult, ALU.add,
                                             gs[:, c:c + 1]).then_inc(s["sg"], 1)

            def wu(i, p, g):
                if g % 7 == 0:
                    dve.wait_ge(s["xb"], at(i, 2, g // 7 + 1))
                dve.wait_ge(s["wu"], at(i, HG, g + 1))
                dve.tensor_tensor(x1[:, p, g:NG:HG, :], ps_w[g % 2][0:GP, 0:2 * C].rearrange("p (a c) -> p a c", a=2),
                                  x1[:, p, g:NG:HG, :], ALU.add).then_inc(s["x1"], 1)
                if g:
                    stats(i, p, g - 1)

            def norm(i, p, _):
                stats(i, p, HG - 1)
                dve.wait_ge(s["sg"], at(i, NG, NG))
                n0 = [0]

                def linked(op):
                    n0[0] += 1
                    op.then_inc(s["st"], 1)
                    dve.wait_ge(s["st"], at(i, 5, n0[0]))

                linked(dve.tensor_tensor(m_s[:, :], st[:, :, 1], st[:, :, 4], ALU.add))
                linked(dve.tensor_tensor(m_d[:, :], st[:, :, 1], st[:, :, 4], ALU.subtract))
                linked(dve.tensor_tensor(m_v[:, :], st[:, :, 2], st[:, :, 5], ALU.add))
                linked(dve.tensor_tensor(m_q[:, :], m_d[:, :], m_d[:, :], ALU.mult))
                linked(dve.tensor_scalar(m_v[:, :], m_v[:, :], 1.0 / C, EPS, ALU.mult, ALU.add))
                dve.scalar_tensor_tensor(var[:, :], m_q[:, :], 0.25, m_v[:, :], ALU.mult, ALU.add).then_inc(s["var"], 1)

            def split(i, p, j):
                if j == 0:
                    dve.wait_ge(s["rstd"], at(i, 1, 1))
                    dve.scalar_tensor_tensor(nmr[:, :], m_s[:, :], -0.5, rstd[:, :], ALU.mult, ALU.mult).then_inc(s["nmr"], 1)
                    dve.tensor_tensor(gr1[:, :], gs[:, :], rstd[:, :], ALU.mult).then_inc(s["gr1"], 1)
                    dve.wait_ge(s["nmr"], at(i, 1, 1))
                    dve.wait_ge(s["gr1"], at(i, 1, 1))
                    wait(dve, s["p1"], i, 1, 0)
                    dve.scalar_tensor_tensor(gray[:, :], nmr[:, :], k["gamma_sum"][:, :], gr1[:, :], ALU.mult, ALU.add).then_inc(s["gray"], 1)
                r = n_par(i, p, j)
                dve.wait_ge(s["hi"], at(i, NT, j + 1))
                dve.tensor_tensor(xs[:, r, :, C:256], xh[:, r, :, 128:C], xs[:, r, :, 128:C], ALU.subtract)
                dve.tensor_tensor(xs[:, r, :, 256:2 * C], xh[:, r, :, 0:128], xs[:, r, :, 0:128], ALU.subtract).then_inc(s["lo"], 1)

            def turn(i, p, j):
                for n in range(3 * j, 3 * j + 3):
                    if n % 2 == 1:
                        dve.wait_ge(s["turn"], at(i, 3 * NT, n + 1))
                        dve.tensor_copy(unit_of(seq[:, p, n % 3, 1:1 + PIX], j),
                                        ps_x[:, 1, 0:TP].rearrange("c (a s) -> c a s", a=2)).then_inc(s["t1"], 1)

            def select(i, p, piece):
                if piece != 3:
                    return
                dve.wait_ge(s["p4"], at(i, 1, 1))
                dve.tensor_tensor(lgt[:, :], ps_s[0:1, 120:124], k["sel_b2"][:, :], ALU.add).then_inc(s["l1"], 1)
                dve.wait_ge(s["l1"], at(i, 1, 1))
                dve.tensor_tensor(cmp[:, 0:1], lgt[:, 1:2], lgt[:, 0:1], ALU.is_gt)
                dve.tensor_tensor(cmp[:, 1:2], lgt[:, 1:2], lgt[:, 2:3], ALU.is_ge)
                dve.tensor_tensor(cmp[:, 2:3], lgt[:, 1:2], lgt[:, 3:4], ALU.is_ge).then_inc(s["l2"], 1)
                dve.wait_ge(s["l2"], at(i, 1, 1))
                wait(dve, s["perm"], i, 1, 0)
                dve.scalar_tensor_tensor(flag[:, :], cmp[:, 0:1], cmp[:, 1:2], cmp[:, 2:3], ALU.mult, ALU.mult).then_inc(s["flag"], 1)

            def taps(i, p, n, m):
                r = n_par(i, p, n)
                dve.wait_ge(s["u"], at(i, MX, NB * n + m + 1))
                dve.scalar_tensor_tensor(u[:, r, m, :], ps_f[:, m, 0:TP], k["dw"][:, m, 0:1], u[:, r, m, :],
                                         ALU.mult, ALU.add).then_inc(s["w"], 1)
                dve.wait_ge(s["w"], at(i, MX, NB * n + m + 1))
                dve.scalar_tensor_tensor(u[:, r, m, :], ps_f[:, m, 2:TP + 2], k["dw"][:, m, 2:3], u[:, r, m, :],
                                         ALU.mult, ALU.add).then_inc(s["v"], 1)

            def out(i, p, n, q):
                step = 2 * n + q
                c = 2 * step
                dve.wait_ge(s["x1b"], at(i, NT, n + 1))
                dve.wait_ge(s["f2"], at(i, 2 * NT, step + 1))
                dve.tensor_tensor(x1[:, p, c:c + 2, :], ps_o[0:GP, 0:2 * C].rearrange("p (a c) -> p a c", a=2),
                                  x1[:, p, c:c + 2, :], ALU.add).then_inc(s["o"], 1)

            def slot(i, p, n, ahead, place):
                if n < NT:
                    taps(i, p, n, 0)
                place("A")
                if n < NT:
                    taps(i, p, n, 1)
                if n:
                    out(i, p, n - 1, 0)
                place("B")
                if n < NT:
                    taps(i, p, n, 2)
                if n:
                    out(i, p, n - 1, 1)
                place("C")

            schedule(dve, slot, {"conv": conv, "wu": wu, "norm": norm, "split": split, "turn": turn, "select": select})


def constants(np):
    diff = np.zeros((GP, 4, GP), np.float32)
    for m in range(GP):
        if m % W != W - 1:
            diff[m + 1, 0, m], diff[m, 0, m] = 1, -1
        if m < W:
            diff[m + W, 1, m], diff[m, 1, m] = 1, -1
        else:
            diff[m, 2, m] = -1
            diff[m - W, 3, m] = 1
    mixs = np.zeros((GP, 2, 4), np.float32)
    each = 1.0 / (C * H * (W - 1))
    mixs[:, 0, :] = [each, 0, 0.4 * each, each]
    mixs[:, 1, :] = [0, each, 0.4 * each, -each]
    return {"ident": np.eye(128, dtype=np.float32), "diff": diff, "mixs": mixs}


def kernel(**inputs):
    import numpy as np
    import concourse.bacc as bacc
    from concourse.bass_utils import run_bass_kernel_spmd

    a = {n: np.asarray(v) for n, v in inputs.items()}
    L0, L1 = "L0_conv_", "L1_conv_"
    col = lambda v: v.reshape(-1, 1)
    row = lambda v: v.reshape(1, -1)
    chan = lambda v: v.reshape(NB, 128).T
    laid = {
        "x": a["x"],
        "WdT0": a[L0 + "Wd"].T[0:128], "WdT1": a[L0 + "Wd"].T[128:], "W1T0": a[L0 + "W1"].T[0:128], "W1T1": a[L0 + "W1"].T[128:],
        "bd": col(a[L0 + "bd"]), "b1": col(a[L0 + "b1"]), "W2": a[L0 + "W2"], "W2T": a[L0 + "W2"].T, "b2": row(a[L0 + "b2"]),
        "tokT": a[L0 + "mask_token"].T, "WuT": a[L0 + "Wu"].T, "bu": row(a[L0 + "bu"]),
        "WhT": a[L0 + "Wh"].reshape(D, D, 9, D).transpose(3, 1, 2, 0).reshape(D, OC),
        "bh": a[L0 + "bh"].reshape(D, D, 9).transpose(1, 2, 0).reshape(1, OC),
        "fc1_0": a[L1 + "fc1_w"][0:128], "fc1_1": a[L1 + "fc1_w"][128:], "fc1_b": chan(a[L1 + "fc1_b"]),
        "gamma": row(a[L1 + "gamma"]), "gamma0": col(a[L1 + "gamma"])[0:128], "gamma1": col(a[L1 + "gamma"])[128:],
        "beta0": col(a[L1 + "beta"])[0:128], "beta1": col(a[L1 + "beta"])[128:],
        "dw_w": a[L1 + "dw_w"].reshape(NB, 128, 3).transpose(1, 0, 2), "dw_b": chan(a[L1 + "dw_b"]),
        "fc2_w": a[L1 + "fc2_w"].reshape(NB, 128, C).transpose(1, 0, 2), "fc2_b": row(a[L1 + "fc2_b"]),
        "sel_w1": a[L1 + "sel_w1"], "sel_b1": col(a[L1 + "sel_b1"]), "sel_w2": a[L1 + "sel_w2"], "sel_b2": row(a[L1 + "sel_b2"]),
        **constants(np),
    }
    nc = bacc.Bacc("TRN2", target_bir_lowering=False, num_devices=1)
    arrays, t = {}, {}
    for name, v in laid.items():
        arrays["in_" + name] = np.ascontiguousarray(v)
        t[name] = nc.dram_tensor("in_" + name, v.shape, F32, kind="ExternalInput").ap()
    out = nc.dram_tensor("out", (B, H, W, C), F32, kind="ExternalOutput").ap()
    t["map"] = nc.dram_tensor("map_scratch", (B, D, PADDED), F32, kind="Internal").ap()
    t["cw"] = nc.dram_tensor("cw_scratch", (B, OC), F32, kind="Internal").ap()
    t["cw_i"] = t["cw"].rearrange("b (c t d) -> b c t d", t=9, d=D)
    t["x_g"] = t["x"].rearrange("b (g r) w c -> b (r w) g c", r=2)
    t["out_g"] = out.rearrange("b (g r) w c -> b (r w) g c", r=2)
    build(nc, t)
    r = run_bass_kernel_spmd(nc, [arrays], core_ids=[0])
    return r.results[0]["out"]
```

```python
from contextlib import ExitStack

import concourse.bass as bass
from concourse import mybir

F32 = mybir.dt.float32
F32R = mybir.dt.float32r
I32 = mybir.dt.int32
ALU = mybir.AluOpType
ACT = mybir.ActivationFunctionType
AX = mybir.AxisListType

B, H, W, C = 32, 56, 56, 192
D = 64
M = 8
DI = 384
NB = DI // 128
SEL = 16
PIX = H * W
GP = 2 * W
NG = PIX // GP
TG = 4
NT = NG // TG
TP = TG * GP
C1 = C - 128
PW = W + 2
PADDED = PW * PW
CR = 7
CT = H // 2 // CR
CP = CR * W
HP = PIX // 2
HG = NG // 2
YW = M + D
TAPW = 9 * D
OC = D * TAPW
CG = 4
assert B == 128 // CG
WCH = CG * 3 * 512
NCH = OC // WCH
XS = PIX + 2
EPS = 1e-5
MT = 2 * NT
PARTS = ((0, 0), (0, 1), (1, 0), (2, 2), (3, 2))


def build(nc, t):
    ctx = ExitStack()
    with ctx:
        def sem(name):
            return ctx.enter_context(nc.semaphore(name))

        def keep(name, shape, dt=F32):
            return ctx.enter_context(nc.sbuf_tensor(name, shape, dt))

        k = {}
        k["ident"] = keep("ident", [128, 128])
        k["w_ad"] = keep("w_ad", [128, 2, 128])
        k["w_ad_r"] = keep("w_ad_r", [128, 4, 128], F32R)
        k["bias_ad"] = keep("bias_ad", [128, 1])
        k["floor_ad"] = keep("floor_ad", [128, 1])
        k["pick"] = keep("pick", [128, YW])
        k["w2raw"] = keep("w2raw", [D, D])
        k["tokT"] = keep("tokT", [D, M])
        k["w2T"] = keep("w2T", [D + 1, D])
        k["ones"] = keep("ones", [M, 112])
        k["pooled"] = keep("pooled", [D + 1, B])
        k["mwf"] = keep("mwf", [D + 1, B])
        k["wu"] = keep("wu", [128, 2 * C])
        k["fc1"] = keep("fc1", [128, 2, DI])
        k["fc1_r"] = keep("fc1_r", [128, 4, DI], F32R)
        k["gamma_c"] = keep("gamma_c", [128, 2])
        k["beta_c"] = keep("beta_c", [128, 2])
        k["fc1_b"] = keep("fc1_b", [128, NB])
        k["dw"] = keep("dw", [128, NB, 3])
        k["dw_b"] = keep("dw_b", [128, NB])
        k["bias3"] = keep("bias3", [128, 3, NB])
        k["tmp3"] = keep("tmp3", [128, 2, NB])
        k["fc2"] = keep("fc2", [128, NB, C])
        k["gamma_r"] = keep("gamma_r", [GP, C])
        k["gamma_sum"] = keep("gamma_sum", [GP, 1])
        k["bu_r"] = keep("bu_r", [GP, C])
        k["fc2b_r"] = keep("fc2b_r", [GP, C])
        k["diff"] = keep("diff", [GP, 4, GP])
        k["mixs"] = keep("mixs", [GP, 2, 4])
        k["sel_w1"] = keep("sel_w1", [4, 128])
        k["sel_b1"] = keep("sel_b1", [128, 1])
        k["sel_w2"] = keep("sel_w2", [128, 4])
        k["sel_b2"] = keep("sel_b2", [1, 4])
        k["expo"] = keep("expo", [GP, NG])

        ahead = {"x_in": [sem("x_in0"), sem("x_in1")], "wh_in": [sem("wh_in0"), sem("wh_in1")]}
        with nc.sbuf_tensor("xa", [GP, 2, NG, C], F32) as ahead["xa"], nc.sbuf_tensor("wh", [D + 1, 2, WCH], F32) as ahead["wh"]:
            setup(nc, t, k, sem, ahead)
            pass_one(nc, t, k, sem, ahead)
            conv_weights(nc, t, k, sem, ahead)
        pass_two(nc, t, k, sem)


def load_wh(sp, t, ahead, j):
    cols = slice(j * WCH, (j + 1) * WCH)
    sp.dma_start(ahead["wh"][0:D, j % 2, :], t["WhT"][:, cols]).then_inc(ahead["wh_in"][j % 2], 16)
    sp.dma_start(ahead["wh"][D:D + 1, j % 2, :], t["bh"][:, cols]).then_inc(ahead["wh_in"][j % 2], 16)


def at(i, per, n):
    return i * per + n


def wait(eng, s, i, per, n):
    v = i * per + n
    if isinstance(v, int) and v <= 0:
        return
    eng.wait_ge(s, v)


def alone(eng, s):
    eng.sem_inc(s, 1)


def setup(nc, t, k, sem, ahead):
    loads = [
        ("ident", k["ident"][:, :]), ("diff", k["diff"][:, :, :]), ("mixs", k["mixs"][:, :, :]),
        ("WdT0", k["w_ad"][:, 0, 0:D]), ("W1T0", k["w_ad"][:, 0, D:128]),
        ("WdT1", k["w_ad"][0:C1, 1, 0:D]), ("W1T1", k["w_ad"][0:C1, 1, D:128]),
        ("WdT1", k["w_ad"][C1:128, 1, 0:D]), ("W1T1", k["w_ad"][C1:128, 1, D:128]),
        ("bd", k["bias_ad"][0:D, :]), ("b1", k["bias_ad"][D:128, :]),
        ("W2", k["w2raw"][:, :]), ("tokT", k["tokT"][:, :]),
        ("W2T", k["w2T"][0:D, :]), ("b2", k["w2T"][D:D + 1, :]),
        ("WuT", k["wu"][0:D, 0:C]), ("WuT", k["wu"][D:128, C:2 * C]),
        ("fc1_0", k["fc1"][:, 0, :]), ("fc1_1", k["fc1"][0:C1, 1, :]), ("fc1_1", k["fc1"][C1:128, 1, :]),
        ("gamma0", k["gamma_c"][:, 0:1]), ("gamma1", k["gamma_c"][0:C1, 1:2]),
        ("gamma1", k["gamma_c"][C1:128, 1:2]),
        ("beta0", k["beta_c"][:, 0:1]), ("beta1", k["beta_c"][0:C1, 1:2]),
        ("fc1_b", k["fc1_b"][:, :]), ("dw_w", k["dw"][:, :, :]), ("dw_b", k["dw_b"][:, :]),
        ("fc2_w", k["fc2"][:, :, :]),
        ("sel_w1", k["sel_w1"][:, 0:SEL]), ("sel_b1", k["sel_b1"][0:SEL, :]),
        ("sel_w2", k["sel_w2"][0:SEL, :]), ("sel_b2", k["sel_b2"][:, :]),
    ]
    rows = [("gamma", k["gamma_r"]), ("bu", k["bu_r"]), ("fc2_b", k["fc2b_r"])]
    weights_in, zeroed, small_mm, chain, parts = (sem(n) for n in ("weights_in", "zeroed", "small_mm", "chain", "parts"))
    total = 16 * (len(loads) + len(rows))
    with nc.psum_tensor("ps_tok", [128, M], F32) as ps_tok, \
            nc.psum_tensor("ps_beta", [128, NB, 1], F32) as ps_beta, nc.Block() as block:

        @block.sync
        def _(sp):
            sp.dma_start(ahead["xa"][:, 0, :, :], t["x_g"][0]).then_inc(ahead["x_in"][0], 16)
            sp.wait_ge(zeroed, 5)
            for name, dst in loads:
                sp.dma_start(dst, t[name]).then_inc(weights_in, 16)
            for name, dst in rows:
                sp.dma_start(dst[:, :], t[name].to_broadcast([GP, C])).then_inc(weights_in, 16)
            sp.dma_start(ahead["xa"][:, 1, :, :], t["x_g"][1]).then_inc(ahead["x_in"][1], 16)

        @block.vector
        def _(dve):
            dve.memset(k["wu"][:, :], 0.0).then_inc(zeroed, 1)
            dve.memset(k["beta_c"][:, :], 0.0).then_inc(zeroed, 1)
            dve.memset(k["sel_w1"][:, :], 0.0).then_inc(zeroed, 1)
            dve.memset(k["sel_b1"][:, :], 0.0).then_inc(zeroed, 1)
            dve.memset(k["sel_w2"][:, :], 0.0).then_inc(zeroed, 1)
            dve.memset(k["pick"][0:D, :], 0.0)
            dve.memset(k["floor_ad"][0:D, :], -3.0e38)
            dve.memset(k["floor_ad"][D:128, :], 0.0)
            dve.memset(k["ones"][:, :], 1.0)
            dve.memset(k["mwf"][D:D + 1, :], 1.0)
            dve.memset(k["expo"][:, :], -0.5)
            dve.wait_ge(weights_in, total)
            dve.wait_ge(small_mm, 1)
            dve.tensor_copy(k["pick"][D:128, 0:M], ps_tok[D:128, :])
            dve.tensor_copy(k["pick"][D:128, M:YW], k["ident"][D:128, D:128])
            dve.tensor_scalar(k["wu"][:, :], k["wu"][:, :], 0.25, None, ALU.mult)
            for c in range(2):
                dve.tensor_scalar(k["fc1"][:, c, :], k["fc1"][:, c, :], k["gamma_c"][:, c:c + 1], None, ALU.mult).then_inc(parts, 1)
            dve.wait_ge(parts, 2)
            for c in range(2):
                dve.tensor_copy(k["fc1_r"][:, 2 * c, :], k["fc1"][:, c, :]).then_inc(parts, 1)
                dve.tensor_copy(k["w_ad_r"][:, 2 * c, :], k["w_ad"][:, c, :]).then_inc(parts, 1)
            dve.wait_ge(parts, 6)
            for c in range(2):
                dve.tensor_tensor(k["fc1_r"][:, 2 * c + 1, :], k["fc1"][:, c, :], k["fc1_r"][:, 2 * c, :].bitcast(F32), ALU.subtract)
                dve.tensor_tensor(k["w_ad_r"][:, 2 * c + 1, :], k["w_ad"][:, c, :], k["w_ad_r"][:, 2 * c, :].bitcast(F32), ALU.subtract)
            dve.reduce_sum(k["gamma_sum"][:, :], k["gamma_r"][:, :], AX.X)
            bp, ws = k["tmp3"][:, 0, :], k["tmp3"][:, 1, :]
            dve.tensor_tensor(bp, ps_beta[:, :, 0], k["fc1_b"][:, :], ALU.add)
            dve.tensor_tensor(ws, k["dw"][:, :, 0], k["dw"][:, :, 1], ALU.add).then_inc(chain, 1)
            dve.wait_ge(chain, 1)
            dve.tensor_tensor(ws, ws, k["dw"][:, :, 2], ALU.add).then_inc(chain, 1)
            dve.wait_ge(chain, 2)
            dve.tensor_tensor(ws, ws, bp, ALU.mult).then_inc(chain, 1)
            dve.wait_ge(chain, 3)
            dve.tensor_tensor(k["bias3"][:, 0, :], ws, k["dw_b"][:, :], ALU.add).then_inc(chain, 1)
            dve.wait_ge(chain, 4)
            dve.tensor_tensor(ws, k["dw"][:, :, 0], bp, ALU.mult).then_inc(chain, 1)
            dve.wait_ge(chain, 5)
            dve.tensor_tensor(k["bias3"][:, 1, :], k["bias3"][:, 0, :], ws, ALU.subtract).then_inc(chain, 1)
            dve.wait_ge(chain, 6)
            dve.tensor_tensor(ws, k["dw"][:, :, 2], bp, ALU.mult).then_inc(chain, 1)
            dve.wait_ge(chain, 7)
            dve.tensor_tensor(k["bias3"][:, 2, :], k["bias3"][:, 0, :], ws, ALU.subtract).then_inc(chain, 1)

        @block.tensor
        def _(pe):
            pe.wait_ge(weights_in, total)
            pe.matmul(ps_tok[D:128, :], k["w2raw"][:, :], k["tokT"][:, :], start=True, stop=True)
            for m in range(NB):
                for c in range(2):
                    mm = pe.matmul(ps_beta[:, m, :], k["fc1"][:, c, m * 128:(m + 1) * 128],
                                   k["beta_c"][:, c:c + 1], start=(c == 0), stop=(c == 1))
            mm.then_inc(small_mm, 1)


def pass_one(nc, t, k, sem, ahead):
    x_v, map_v = t["x_g"], t["map"]
    with ExitStack() as ctx:
        def sb(name, shape, dt=F32):
            return ctx.enter_context(nc.sbuf_tensor(name, shape, dt))

        def ps(name, shape):
            return ctx.enter_context(nc.psum_tensor(name, shape, F32))

        xa, x_in = ahead["xa"], ahead["x_in"]
        xT = sb("xT", [128, 2, 3, TP], F32R)
        y = sb("y", [128, 2, TP])
        th = sb("th", [D, 2, TP])
        pad = sb("pad", [D, 2, PADDED])
        yl = sb("yl", [GP, 2, NG, YW + 1])
        mx = sb("mx", [GP, M])
        mx8 = sb("mx8", [M, 1])
        dg = sb("dg", [M, M])
        lg = sb("lg", [GP, NG, M])
        ex = sb("ex", [GP, NG, M])
        rz = sb("rz", [M, 1])
        pn = sb("pn", [M, D + 1])
        ps_c0 = ps("ps_c0", [128, 2, 512])
        ps_c1 = ps("ps_c1", [128, 2, 512])
        ps_a = ps("ps_a", [128, 2, 512])
        ps_y = ps("ps_y", [128, 512])
        ps_q = ps("ps_q", [128, 512])
        turned, high, low = sem("turned"), sem("high"), sem("low")
        past, th_one = sem("pool_past1"), sem("th_one")
        proj, y_ready, th_ready, map_ready = sem("proj"), sem("y_ready"), sem("th_ready"), sem("map_ready")
        picked, yl_ready = sem("picked"), sem("yl_ready")
        map_out = [sem("map_out0"), sem("map_out1")]
        q_max, q_turn, q_m8, q_diag, q_bc, q_sub, q_exp = (sem("q_" + n) for n in ("max", "turn", "m8", "diag", "bc", "sub", "exp"))
        q_pool, q_rz, q_norm, q_sum, q_done = (sem("q_" + n) for n in ("pool", "rz", "norm", "sum", "done"))
        border = sem("border")
        block = ctx.enter_context(nc.Block())
        ident = k["ident"]

        def schedule(eng, stages, pool):
            def step(i, p, n):
                for lag, stage in stages:
                    if n >= lag:
                        here(stage, i, p, n - lag)
                    else:
                        here(stage, i - 1, 1 - p, n - lag + NT)
                if pool and n <= 2:
                    here(pool, i - 2, p, n + NT - 2)
                if pool and n >= 2:
                    here(pool, i - 1, 1 - p, n - 2)

            def here(stage, i, p, n):
                if not isinstance(i, int) or 0 <= i < B:
                    stage(i, p, n)

            def image(i, p):
                for n in range(NT):
                    step(i, p, n)

            image(0, 0)
            image(1, 1)
            with eng.Fori(2, B - 1, 2) as i:
                image(i, 0)
                image(i + 1, 1)
            image(B, 0)
            for n in range(3):
                step(B + 1, 1, n)

        @block.sync
        def _(sp):
            def step(i, p, more):
                if more:
                    sp.wait_ge(turned, at(i, MT, MT))
                    sp.dma_start(xa[:, p, :, :], x_v[i + 2]).then_inc(x_in[p], 16)
                sp.wait_ge(map_ready, at(i, NT, NT))
                sp.dma_start(map_v[i], pad[:, p, :]).then_inc(map_out[p], 16)

            with sp.Fori(0, B - 3, 2) as i:
                step(i, 0, True)
                step(i + 1, 1, True)
            for j in range(2):
                load_wh(sp, t, ahead, j)
            step(B - 2, 0, False)
            step(B - 1, 1, False)
            for p in range(2):
                sp.wait_ge(map_out[p], 16 * B // 2)

        @block.tensor
        def _(pe):
            def turn(i, p, n):
                if n == 0:
                    pe.wait_ge(x_in[p], (i - p) * 8 + 16)
                wait(pe, low, i, MT, 2 * (n - 1))
                r = n_par(i, p, n)
                px = [slice(g * GP, (g + 1) * GP) for g in range(TG)]
                for g in range(TG):
                    tr = pe.transpose(ps_c0[:, r, px[g]], xa[:, p, n * TG + g, 0:128], ident[0:GP, 0:GP])
                tr.then_inc(turned, 1)
                for g in range(TG):
                    tr = pe.transpose(ps_c1[0:C1, r, px[g]], xa[:, p, n * TG + g, 128:C], ident[0:GP, 0:GP])
                tr.then_inc(turned, 1)

            def project(i, p, n):
                r = n_par(i, p, n)
                pe.wait_ge(low, at(i, MT, 2 * (n + 1)))
                wait(pe, y_ready, i, NT, n - 1)
                for q, (w, c) in enumerate(PARTS):
                    mm = pe.matmul(ps_a[:, r, 0:TP], k["w_ad_r"][:, w, :], xT[:, r, c, :], start=(q == 0), stop=(q == len(PARTS) - 1))
                mm.then_inc(proj, 1)

            def pick(i, p, n):
                r = n_par(i, p, n)
                pe.wait_ge(y_ready, at(i, NT, n + 1))
                wait(pe, yl_ready, i, NT, n)
                for g in range(TG):
                    mm = pe.matmul(ps_y[0:GP, g * YW:(g + 1) * YW], y[:, r, g * GP:(g + 1) * GP], k["pick"][:, :], start=True, stop=True)
                mm.then_inc(picked, 1)

            def pool(i, p, slot):
                if slot == 1:
                    pe.wait_ge(q_max, at(i, 1, 1))
                    pe.transpose(ps_q[0:M, 0:GP], mx[:, :], ident[0:GP, 0:GP]).then_inc(q_turn, 1)
                if slot == 2:
                    pe.wait_ge(q_diag, at(i, 1, 1))
                    pe.matmul(ps_q[0:GP, 128:128 + M], k["ones"][:, :], dg[:, :], start=True, stop=True).then_inc(q_bc, 1)
                if slot == 4:
                    pe.wait_ge(q_exp, at(i, 1, 1))
                    for g in range(NG):
                        mm = pe.matmul(ps_q[0:M, 160:160 + D + 1], ex[:, g, :], yl[:, p, g, M:YW + 1], start=(g == 0), stop=(g == NG - 1))
                    mm.then_inc(q_pool, 1)
                if slot == 6:
                    pe.wait_ge(q_norm, at(i, 1, 1))
                    pe.matmul(ps_q[0:D + 1, 256:257], pn[:, :], k["ones"][:, 0:1], start=True, stop=True).then_inc(q_sum, 1)

            schedule(pe, [(0, turn), (1, project), (2, pick)], pool)

        @block.scalar
        def _(act):
            def round_x(i, p, n):
                r = n_par(i, p, n)
                wait(act, proj, i, NT, n - 1)
                for c, ps_c in enumerate((ps_c0, ps_c1)):
                    act.wait_ge(turned, at(i, MT, 2 * n + c + 1))
                    cs = slice(0, (128, C1)[c])
                    act.activation(xT[cs, r, 2 * c, :], ps_c[cs, r, 0:TP], ACT.Copy).then_inc(high, 1)

            def tanh(i, p, n):
                r = n_par(i, p, n)
                act.wait_ge(y_ready, at(i, NT, n + 1))
                wait(act, map_ready, i, NT, n - 1)
                act.activation(th[:, r, :], y[0:D, r, :], ACT.Tanh, scale=0.851).then_inc(th_ready, 1)

            def evac_y(i, p, n):
                act.wait_ge(picked, at(i, NT, n + 1))
                if n == 0:
                    wait(act, q_pool, i, 1, -1)
                act.activation(yl[:, p, n * TG:(n + 1) * TG, 0:YW],
                               ps_y[0:GP, 0:TG * YW].rearrange("p (g w) -> p g w", w=YW), ACT.Copy).then_inc(yl_ready, 1)

            def pool(i, p, slot):
                if slot == 3:
                    act.wait_ge(q_sub, at(i, 1, 1))
                    wait(act, q_pool, i, 1, 0)
                    act.activation(ex[:, :, :], lg[:, :, :], ACT.Exp).then_inc(q_exp, 1)

            schedule(act, [(0, round_x), (2, evac_y), (1, tanh)], pool)

        @block.vector
        def _(dve):
            dve.memset(pad[:, :, :], 0.0).then_inc(border, 1)
            dve.memset(yl[:, :, :, YW:YW + 1], 1.0).then_inc(border, 1)
            dve.wait_ge(border, 2)

            def rest_of_x(i, p, n):
                r = n_par(i, p, n)
                for c, ps_c in enumerate((ps_c0, ps_c1)):
                    cs = slice(0, (128, C1)[c])
                    dve.wait_ge(high, at(i, MT, 2 * n + c + 1))
                    dve.tensor_tensor(xT[C1 * c:128, r, 1 + c, :], ps_c[cs, r, 0:TP], xT[cs, r, 2 * c, :].bitcast(F32),
                                      ALU.subtract).then_inc(low, 1)

            def biased(i, p, n):
                r = n_par(i, p, n)
                dve.wait_ge(proj, at(i, NT, n + 1))
                wait(dve, picked, i, NT, n - 1)
                wait(dve, map_ready, i, NT, n - 1)
                dve.tensor_scalar(y[:, r, :], ps_a[:, r, 0:TP], k["bias_ad"][:, :], k["floor_ad"][:, :],
                                  ALU.add, ALU.max).then_inc(y_ready, 1)

            def pool(i, p, slot):
                if slot == 0:
                    dve.wait_ge(yl_ready, at(i, NT, NT))
                    wait(dve, q_turn, i, 1, 0)
                    dve.tensor_reduce(mx[:, :], yl[:, p, :, 0:M].rearrange("p g m -> p m g"), AX.X, ALU.max).then_inc(q_max, 1)
                if slot == 1:
                    dve.wait_ge(q_turn, at(i, 1, 1))
                    dve.tensor_reduce(mx8[:, :], ps_q[0:M, 0:GP], AX.X, ALU.max).then_inc(q_m8, 1)
                    dve.wait_ge(q_m8, at(i, 1, 1))
                    dve.tensor_scalar(dg[:, :], ident[0:M, 0:M], mx8[:, :], None, ALU.mult).then_inc(q_diag, 1)
                if slot == 2:
                    dve.wait_ge(q_bc, at(i, 1, 1))
                    dve.tensor_tensor(lg[:, :, :].rearrange("p g m -> p m g"), yl[:, p, :, 0:M].rearrange("p g m -> p m g"),
                                      ps_q[0:GP, 128:128 + M].unsqueeze(2).to_broadcast([GP, M, NG]), ALU.subtract).then_inc(q_sub, 1)
                if slot == 4:
                    dve.wait_ge(q_pool, at(i, 1, 1))
                    dve.reciprocal(rz[:, :], ps_q[0:M, 160 + D:161 + D]).then_inc(q_rz, 1)
                    dve.wait_ge(q_rz, at(i, 1, 1))
                    dve.tensor_scalar(pn[:, :], ps_q[0:M, 160:161 + D], rz[:, :], None, ALU.mult).then_inc(q_norm, 1)
                if slot == 7:
                    dve.wait_ge(q_sum, at(i, 1, 1))
                    dve.tensor_copy(k["pooled"][:, bass.ds(i, 1)], ps_q[0:D + 1, 256:257]).then_inc(q_done, 1)

            schedule(dve, [(0, rest_of_x), (1, biased)], pool)

        @block.gpsimd
        def _(pool):
            def gelu_map(i, p, n):
                r = n_par(i, p, n)
                pool.wait_ge(th_ready, at(i, NT, n + 1))
                if n == 0 and not (isinstance(i, int) and i < 2):
                    pool.wait_ge(map_out[p], (i - p) * 8)
                alone(pool, past)
                rows = pad[:, p, PW + n * (TP // W) * PW:PW + (n + 1) * (TP // W) * PW].rearrange("c (h w) -> c h w", w=PW)
                pool.tensor_scalar(th[:, r, :], th[:, r, :], 1.0, None, ALU.add).then_inc(th_one, 1)
                pool.wait_ge(th_one, at(i, NT, n + 1))
                alone(pool, past)
                pool.tensor_tensor(rows[:, :, 1:W + 1], th[:, r, :].rearrange("c (h w) -> c h w", w=W),
                                   y[0:D, r, :].rearrange("c (h w) -> c h w", w=W), ALU.mult).then_inc(map_ready, 1)

            pool.wait_ge(border, 2)
            schedule(pool, [(0, gelu_map)], None)


def n_par(i, p, n):
    return (p * NT + n) % 2


def conv_weights(nc, t, k, sem, ahead):
    with ExitStack() as ctx:
        wh, wh_in = ahead["wh"], ahead["wh_in"]
        cwo = ctx.enter_context(nc.sbuf_tensor("cwo", [CG * B, 2, WCH // CG], F32))
        ps_m = ctx.enter_context(nc.psum_tensor("ps_m", [128, 512], F32))
        ps_h = ctx.enter_context(nc.psum_tensor("ps_h", [128, 4, 512], F32))
        mwf_mm, mwf_ready, hyper, hyper_out = (sem(n) for n in ("mwf_mm", "mwf_ready", "hyper", "hyper_out"))
        cw_out = [sem("cw_out0"), sem("cw_out1")]
        N = WCH // CG // 512
        QW = WCH // CG
        block = ctx.enter_context(nc.Block())

        @block.sync
        def _(sp):
            for j in range(NCH + 2):
                if 2 <= j < NCH:
                    sp.wait_ge(hyper, N * (j - 1))
                    load_wh(sp, t, ahead, j)
                if j >= 2:
                    sp.wait_ge(hyper_out, N * (j - 1))
                    for q in range(CG):
                        o = (j - 2) * WCH + q * QW
                        sp.dma_start(t["cw"][:, o:o + QW], cwo[q * B:(q + 1) * B, j % 2, :]).then_inc(cw_out[j % 2], 16)
            for r in range(2):
                sp.wait_ge(cw_out[r], 16 * CG * NCH // 2)

        @block.tensor
        def _(pe):
            pe.matmul(ps_m[0:D, 0:B], k["w2T"][:, :], k["pooled"][:, :], start=True, stop=True).then_inc(mwf_mm, 1)
            pe.wait_ge(mwf_ready, 1)
            for j in range(NCH):
                pe.wait_ge(wh_in[j % 2], 32 * (j // 2 + 1))
                for n in range(N):
                    s = j * N + n
                    if s >= 4:
                        pe.wait_ge(hyper_out, s - 3)
                    for q in range(CG):
                        o = q * QW + n * 512
                        mm = pe.matmul(ps_h[q * B:(q + 1) * B, s % 4, :], k["mwf"][:, :], wh[:, j % 2, o:o + 512],
                                       start=True, stop=True)
                    mm.then_inc(hyper, 1)

        @block.vector
        def _(dve):
            dve.wait_ge(mwf_mm, 1)
            dve.tensor_copy(k["mwf"][0:D, :], ps_m[0:D, 0:B]).then_inc(mwf_ready, 1)
            for j in range(NCH):
                if j >= 2:
                    dve.wait_ge(cw_out[j % 2], 16 * CG * (j // 2))
                for n in range(N):
                    s = j * N + n
                    dve.wait_ge(hyper, s + 1)
                    dve.tensor_copy(cwo[:, j % 2, n * 512:(n + 1) * 512], ps_h[:, s % 4, :]).then_inc(hyper_out, 1)


PLAN = {
    (0, "A"): [("conv", 0)], (0, "C"): [("wu", 0)], (0, "D"): [("conv", 1)], (0, "E"): [("wu", 1)],
    (1, "B"): [("wu", 2)], (1, "C"): [("wu", 3)], (1, "D"): [("wu", 4), ("conv", 2), ("wu", 5)],
    (1, "E"): [("wu", 6)],
    (2, "A"): [("wu", 7)], (2, "B"): [("wu", 8)], (2, "C"): [("conv", 3), ("wu", 9)],
    (2, "D"): [("norm", 0), ("wu", 10)], (2, "E"): [("wu", 11)],
    (3, "A"): [("shift", 0)], (3, "D"): [("wu", 12), ("wu", 13), ("norm", 1), ("turn", 0)],
    (4, "A"): [("turn", 1)], (4, "B"): [("turn", 2)], (4, "D"): [("turn", 3), ("turn", 4)],
    (4, "E"): [("shift", 1), ("turn", 5)],
    (5, "B"): [("select", 0), ("turn", 6)], (5, "C"): [("select", 1)], (5, "D"): [("turn", 7), ("turn", 8)],
    (6, "A"): [("select", 2), ("turn", 9)], (6, "D"): [("turn", 10), ("select", 3), ("turn", 11)],
    (6, "E"): [("turn", 12)],
    (7, "C"): [("turn", 13)],
}
FIRST = 8
SLOTS = NT + 1
PLACES = "ABCDE"


def pass_two(nc, t, k, sem):
    x_v, map_v, cw_v, out_v = t["x_g"], t["map"], t["cw_i"], t["out_g"]
    with ExitStack() as ctx:
        def sb(name, shape, dt=F32):
            return ctx.enter_context(nc.sbuf_tensor(name, shape, dt))

        def ps(name, shape):
            return ctx.enter_context(nc.psum_tensor(name, shape, F32))

        x1 = sb("x1", [GP, 2, NG, C])
        pads = sb("pads", [128, PADDED])
        cw = sb("cw_s", [128, 6, D])
        tc = sb("tc", [128, 2, CP])
        xd2 = sb("xd2", [128, HP])
        st = sb("st", [GP, NG, 6])
        gs = sb("gs", [GP, NG])
        junk = sb("junk", [GP, 2, C])
        m_s, m_d, m_v, m_q, var = (sb(n, [GP, NG]) for n in ("m_s", "m_d", "m_v", "m_q", "var"))
        rstd = sb("rstd", [GP, NG])
        nmr = sb("nmr", [GP, NG])
        gr1 = sb("gr1", [GP, NG])
        gray = sb("gray", [GP, NG])
        absd = sb("absd", [GP, 2, 2 * NG])
        hv = sb("hv", [GP, 2])
        sc4 = sb("sc4", [4, 1])
        hid = sb("hid", [128, 1])
        lgt = sb("lgt", [1, 4])
        cmp = sb("cmp", [1, 4])
        flag = sb("flag", [1, 1], I32)
        xh = sb("xh", [GP, 2, TG, C])
        seq = sb("seq", [128, 2, 3, XS], F32R)
        ug = sb("ug", [128, 2, 2, NB, TP])
        u, gl = ug[:, 0], ug[:, 1]
        spare = ug[:, :, :, :, :].rearrange("c a b m s -> c (a b m s)")[:, 0:PIX]
        ps_x = ps("ps_x", [128, 2, 512])
        ps_w0 = ps("ps_w0", [128, 512])
        ps_w1 = ps("ps_w1", [128, 512])
        ps_o = ps("ps_o", [128, 512])
        ps_f = ps("ps_f", [128, NB, 512])
        ps_w, ps_s = [ps_w0, ps_w1], ps_w1
        s = {n: sem("t_" + n) for n in (
            "xb", "conv", "th", "xd", "wu", "x1", "sg", "st", "var", "rstd", "nmr", "gr1", "gray",
            "p1", "hv", "p2", "sc4", "p3", "hid", "p4", "l1", "l2", "flag", "xh", "hi", "lo", "x1b", "turn",
            "perm", "f1", "u", "w", "v", "g", "f2", "o", "zero", "vcopy", "pool_past", "pe_past")}
        cin = sem("cin")
        x_in = [sem("x2_in0"), sem("x2_in1")]
        outs = [sem("outs0"), sem("outs1")]
        block = ctx.enter_context(nc.Block())
        ident = k["ident"]
        MX = NT * NB

        def schedule(eng, slot, item):
            def items(i, p, n, place):
                for what, j in PLAN.get((n, place), []):
                    item[what](i, p, j)

            def turn_of(i, p, ahead):
                for n in range(SLOTS):
                    slot(i, p, n, ahead is not None, lambda place, n=n: items(ahead, 1 - p, n, place) if ahead is not None else None)

            for n in range(SLOTS):
                for place in PLACES:
                    items(0, 0, n, place)
            turn_of(0, 0, 1)
            with eng.Fori(1, B - 2, 2) as i:
                turn_of(i, 1, i + 1)
                turn_of(i + 1, 0, i + 2)
            turn_of(B - 1, 1, None)

        def nothing(i, p, j):
            pass

        def part(stat, h):
            return stat[:, :].rearrange("p (a g) -> p a g", a=2)[:, :, (0, FIRST)[h]:(FIRST, HG)[h]]

        @block.sync
        def _(sp):
            def load_conv(i):
                sp.dma_start(pads[0:D, :], map_v[i]).then_inc(cin, 16)
                sp.dma_start(pads[D:128, 0:PADDED - PW], map_v[i][:, PW:PADDED]).then_inc(cin, 16)
                sp.dma_start(cw[0:D, 0:3, :], cw_v[i][:, 0:3, :]).then_inc(cin, 16)
                sp.dma_start(cw[D:128, :, :], cw_v[i][:, 3:9, :]).then_inc(cin, 16)

            def load_x(i, p, h):
                for a in range(2):
                    g = a * HG + h * 7
                    sp.dma_start(x1[:, p, g:g + 7, :], x_v[i][:, g:g + 7, :]).then_inc(x_in[h], 16)

            def turn_of(i, p, conv_next, x_next):
                for n in range(NT):
                    if n == 3 and conv_next:
                        sp.wait_ge(s["conv"], at(i, CT, 2 * CT))
                        load_conv(i + 2)
                    if n == NT - 1 and x_next:
                        sp.wait_ge(outs[p], (i - p) * (8 * NT) + 16 * (NT - 1))
                        load_x(i + 2, p, 0)
                    sp.wait_ge(s["o"], at(i, 2 * NT, 2 * n + 2))
                    sp.dma_start(out_v[i][:, n * TG:(n + 1) * TG, :], x1[:, p, n * TG:(n + 1) * TG, :]).then_inc(outs[p], 16)
                if x_next:
                    sp.wait_ge(outs[p], (i - p) * (8 * NT) + 16 * NT)
                    load_x(i + 2, p, 1)

            sp.wait_ge(s["zero"], 1)
            load_conv(0)
            for h in range(2):
                load_x(0, 0, h)
            for h in range(2):
                sp.wait_ge(x_in[h], 32)
                load_x(1, 1, h)
            sp.wait_ge(s["conv"], CT)
            load_conv(1)
            turn_of(0, 0, True, True)
            with sp.Fori(1, B - 4, 2) as i:
                turn_of(i, 1, True, True)
                turn_of(i + 1, 0, True, True)
            turn_of(B - 3, 1, True, True)
            turn_of(B - 2, 0, False, False)
            turn_of(B - 1, 1, False, False)
            for p in range(2):
                sp.wait_ge(outs[p], 16 * NT * B // 2)

        @block.gpsimd
        def _(pool):
            def add_bu(i, p, h):
                pool.wait_ge(x_in[h], at(i, 32, 32))
                alone(pool, s["pool_past"])
                for a in range(2):
                    g = a * HG + h * 7
                    op = pool.tensor_tensor(x1[:, p, g:g + 7, :], x1[:, p, g:g + 7, :],
                                            k["bu_r"][:, :].unsqueeze(1).to_broadcast([GP, 7, C]), ALU.add)
                op.then_inc(s["xb"], 1)

            def normalise(i, p, h):
                pool.wait_ge(s["var"], at(i, 2, h + 1))
                wait(pool, s["gray"], i, 1, 0)
                wait(pool, s["xh"], i, NT, 0)
                pool.tensor_tensor(part(rstd, h), part(var, h), part(k["expo"], h), ALU.pow).then_inc(s["rstd"], 1)
                pool.wait_ge(s["nmr"], at(i, 2, h + 1))
                pool.wait_ge(s["rstd"], at(i, 2, h + 1))
                for j in (range(FIRST // 2), range(FIRST // 2, NT))[h]:
                    r = n_par(i, p, j)
                    wait(pool, s["turn"], i, MT, 2 * (j - 1))
                    alone(pool, s["pool_past"])
                    for g in range(TG):
                        c = (g // 2) * HG + 2 * j + g % 2
                        op = pool.tensor_scalar(xh[:, r, g, :], x1[:, p, c, :], rstd[:, c:c + 1], nmr[:, c:c + 1],
                                                ALU.mult, ALU.add)
                    op.then_inc(s["xh"], 1)

            def column_order(i, p):
                pool.wait_ge(s["lo"], at(i, MT, MT))
                pool.wait_ge(s["flag"], at(i, 1, 1))
                alone(pool, s["pool_past"])
                by_column = pool.value_load(flag[0:1, 0:1], min_val=0, max_val=1)
                with pool.If(by_column):
                    wait(pool, s["f2"], i, 2 * NT, 0)
                    for c in range(3):
                        if c:
                            pool.wait_ge(s["vcopy"], at(i, 6, 2 * c))
                        alone(pool, s["pool_past"])
                        rows = seq[:, p, c, 1:1 + PIX]
                        pool.tensor_copy(spare.rearrange("c (w h) -> c w h", h=H),
                                         rows.bitcast(F32).rearrange("c (h w) -> c w h", w=W)).then_inc(s["vcopy"], 1)
                        pool.wait_ge(s["vcopy"], at(i, 6, 2 * c + 1))
                        alone(pool, s["pool_past"])
                        pool.tensor_copy(rows, spare).then_inc(s["vcopy"], 1)
                with pool.Else():
                    pool.sem_inc(s["vcopy"], 6)
                pool.wait_ge(s["vcopy"], at(i, 6, 6))
                pool.sem_inc(s["perm"], 1)

            def add_fc2b(i, p, tiles):
                if tiles[0] == 0:
                    pool.wait_ge(s["xh"], at(i, NT, NT))
                    pool.wait_ge(s["perm"], at(i, 1, 1))
                for n in tiles:
                    c = n * TG
                    pool.tensor_tensor(x1[:, p, c:c + TG, :], x1[:, p, c:c + TG, :],
                                       k["fc2b_r"][:, :].unsqueeze(1).to_broadcast([GP, TG, C]), ALU.add).then_inc(s["x1b"], 1)

            def turn_of(i, p, ahead):
                if ahead is not None:
                    add_bu(ahead, 1 - p, 0)
                add_fc2b(i, p, range(0, 2))
                if ahead is not None:
                    add_bu(ahead, 1 - p, 1)
                add_fc2b(i, p, range(2, NT))
                if ahead is not None:
                    normalise(ahead, 1 - p, 0)
                    normalise(ahead, 1 - p, 1)
                    column_order(ahead, 1 - p)

            for h in range(2):
                add_bu(0, 0, h)
            normalise(0, 0, 0)
            normalise(0, 0, 1)
            column_order(0, 0)
            turn_of(0, 0, 1)
            with pool.Fori(1, B - 2, 2) as i:
                turn_of(i, 1, i + 1)
                turn_of(i + 1, 0, i + 2)
            turn_of(B - 1, 1, None)

        @block.tensor
        def _(pe):
            def conv(i, p, n):
                if n == 0:
                    pe.wait_ge(cin, at(i, 64, 64))
                    wait(pe, s["lo"], i, MT, 0)
                wait(pe, s["xd"], i, CT, n - 1)
                for tap in range(6):
                    down = tap // 3
                    for half in range(2):
                        o = (half * H // 2 + n * CR + down) * PW
                        mv = pads[:, o:o + CR * PW].rearrange("c (h w) -> c h w", w=PW)[:, :, tap % 3:tap % 3 + W]
                        mm = pe.matmul(ps_x[half * D:(half + 1) * D, n % 2, 0:CP], cw[:, tap, :], mv,
                                       start=(tap == 0), stop=(tap == 5))
                mm.then_inc(s["conv"], 1)

            def wu(i, p, g):
                pe.wait_ge(s["xd"], at(i, CT, (g * GP + GP - 1) // CP + 1))
                if g == 0:
                    wait(pe, s["flag"], i, 1, 0)
                wait(pe, s["x1"], i, HG, g - 1)
                pe.matmul(ps_w[g % 2][0:GP, 0:2 * C], xd2[:, g * GP:(g + 1) * GP], k["wu"][:, :],
                          start=True, stop=True).then_inc(s["wu"], 1)

            def select(i, p, piece):
                if piece == 0:
                    pe.wait_ge(s["gray"], at(i, 1, 1))
                    pe.wait_ge(s["x1"], at(i, HG, HG))
                    pe.matmul(ps_s[0:GP, 0:NG], k["diff"][:, 0, :], gray[:, :], start=True, stop=True)
                    pe.matmul(ps_s[0:GP, NG:2 * NG], k["diff"][:, 1, :], gray[:, :], start=True, stop=True)
                    pe.matmul(ps_s[0:GP, 2 * NG:3 * NG - 1], k["diff"][:, 2, :], gray[:, 0:NG - 1], start=True, stop=False)
                    pe.matmul(ps_s[0:GP, 2 * NG:3 * NG - 1], k["diff"][:, 3, :], gray[:, 1:NG], start=False, stop=True).then_inc(s["p1"], 1)
                if piece == 1:
                    pe.wait_ge(s["hv"], at(i, 1, 1))
                    pe.matmul(ps_s[0:4, 100:101], k["mixs"][:, 0, :], hv[:, 0:1], start=True, stop=False)
                    pe.matmul(ps_s[0:4, 100:101], k["mixs"][:, 1, :], hv[:, 1:2], start=False, stop=True).then_inc(s["p2"], 1)
                if piece == 2:
                    pe.wait_ge(s["sc4"], at(i, 1, 1))
                    pe.matmul(ps_s[:, 110:111], k["sel_w1"][:, :], sc4[:, :], start=True, stop=True).then_inc(s["p3"], 1)
                if piece == 3:
                    pe.wait_ge(s["hid"], at(i, 1, 1))
                    pe.matmul(ps_s[0:1, 120:124], hid[:, :], k["sel_w2"][:, :], start=True, stop=True).then_inc(s["p4"], 1)

            def turn(i, p, n):
                j, c = n // 2, n % 2
                r = n_par(i, p, j)
                pe.wait_ge(s["xh"], at(i, NT, j + 1))
                wait(pe, s["lo"], i, MT, n - 1)
                if c:
                    alone(pe, s["pe_past"])
                for g in range(TG):
                    px = slice(g * GP, (g + 1) * GP)
                    cs = slice(0, (128, C1)[c])
                    tr = pe.transpose(ps_x[cs, c, px], xh[:, r, g, (0, 128)[c]:(128, C)[c]], ident[0:GP, 0:GP])
                tr.then_inc(s["turn"], 1)

            def fc1(i, p, n, m):
                if n == 0 and m == 0:
                    pe.wait_ge(s["perm"], at(i, 1, 1))
                wait(pe, s["v"], i, MX, NB * n + m - 2)
                cols = slice(m * 128, (m + 1) * 128)
                at_ = slice(n * TP, n * TP + TP + 2)
                for q, (w, c) in enumerate(PARTS):
                    mm = pe.matmul(ps_f[:, m, 0:TP + 2], k["fc1_r"][:, w, cols], seq[:, p, c, at_],
                                   start=(q == 0), stop=(q == len(PARTS) - 1))
                mm.then_inc(s["f1"], 1)

            def fc2(i, p, n, q):
                r = n_par(i, p, n)
                pe.wait_ge(s["g"], at(i, MX, NB * (n + 1)))
                wait(pe, s["o"], i, 2 * NT, 2 * n + q)
                for g in range(2):
                    for m in range(NB):
                        a = (2 * q + g) * GP
                        mm = pe.matmul(ps_o[0:GP, g * C:(g + 1) * C], gl[:, r, m, a:a + GP], k["fc2"][:, m, :],
                                       start=(m == 0), stop=(m == NB - 1))
                mm.then_inc(s["f2"], 1)

            def slot(i, p, n, ahead, place):
                if n < NT:
                    fc1(i, p, n, 0)
                place("A")
                if n < NT:
                    fc1(i, p, n, 1)
                place("B")
                if n < NT:
                    fc1(i, p, n, 2)
                place("C")
                if n:
                    fc2(i, p, n - 1, 0)
                place("D")
                if n:
                    fc2(i, p, n - 1, 1)
                place("E")

            schedule(pe, slot, {"conv": conv, "wu": wu, "norm": nothing, "shift": nothing,
                                "turn": turn, "select": select})

        def unit_of(ap, j):
            return ap.rearrange("c (a s) -> c a s", a=2)[:, :, 2 * j * GP:2 * (j + 1) * GP]

        def tile_of(ap):
            return ap.rearrange("c (a s) -> c a s", a=2)

        @block.scalar
        def _(act):
            def conv(i, p, n):
                act.wait_ge(s["conv"], at(i, CT, n + 1))
                wait(act, s["xd"], i, CT, n - 1)
                act.activation(tc[:, n % 2, :], ps_x[:, n % 2, 0:CP], ACT.Tanh, scale=0.4255).then_inc(s["th"], 1)

            def select(i, p, piece):
                if piece == 0:
                    act.wait_ge(s["p1"], at(i, 1, 1))
                    act.activation(absd[:, 0, 0:NG], ps_s[0:GP, 0:NG], ACT.Abs, accum_out=hv[:, 0:1])
                    act.activation(absd[:, 1, 0:2 * NG - 1], ps_s[0:GP, NG:3 * NG - 1], ACT.Abs, accum_out=hv[:, 1:2]).then_inc(s["hv"], 1)
                if piece == 1:
                    act.wait_ge(s["p2"], at(i, 1, 1))
                    act.activation(sc4[:, :], ps_s[0:4, 100:101], ACT.Abs).then_inc(s["sc4"], 1)
                if piece == 2:
                    act.wait_ge(s["p3"], at(i, 1, 1))
                    act.activation(hid[:, :], ps_s[:, 110:111], ACT.Relu, bias=k["sel_b1"][:, :]).then_inc(s["hid"], 1)

            def turn(i, p, n):
                j, c = n // 2, n % 2
                act.wait_ge(s["turn"], at(i, MT, n + 1))
                cs = slice(0, (128, C1)[c])
                act.activation(unit_of(seq[cs, p, 2 * c, 1:1 + PIX], j), tile_of(ps_x[cs, c, 0:TP]), ACT.Copy).then_inc(s["hi"], 1)

            def middle(i, p, n, m):
                r = n_par(i, p, n)
                act.wait_ge(s["f1"], at(i, MX, NB * n + m + 1))
                w1, b = k["dw"][:, m, 1:2], k["bias3"]
                lo, hi = (1 if n == 0 else 0), (TP - 1 if n == NT - 1 else TP)
                if n == 0:
                    act.activation(u[:, r, m, 0:1], ps_f[:, m, 1:2], ACT.Identity, scale=w1, bias=b[:, 1, m:m + 1])
                if n == NT - 1:
                    act.activation(u[:, r, m, TP - 1:TP], ps_f[:, m, TP:TP + 1], ACT.Identity, scale=w1, bias=b[:, 2, m:m + 1])
                act.activation(u[:, r, m, lo:hi], ps_f[:, m, 1 + lo:1 + hi], ACT.Identity, scale=w1,
                               bias=b[:, 0, m:m + 1]).then_inc(s["u"], 1)

            def gelu(i, p, n, m):
                r = n_par(i, p, n)
                act.wait_ge(s["v"], at(i, MX, NB * n + m + 1))
                wait(act, s["f2"], i, 2 * NT, 2 * n - 2)
                act.activation(gl[:, r, m, :], u[:, r, m, :], ACT.Gelu).then_inc(s["g"], 1)

            def slot(i, p, n, ahead, place):
                if n < NT:
                    wait(act, s["g"], i, MX, NB * (n - 1))
                    middle(i, p, n, 0)
                place("A")
                if n < NT:
                    middle(i, p, n, 1)
                place("B")
                if n < NT:
                    middle(i, p, n, 2)
                place("C")
                if n < NT:
                    gelu(i, p, n, 0)
                place("D")
                if n < NT:
                    gelu(i, p, n, 1)
                    gelu(i, p, n, 2)
                place("E")

            schedule(act, slot, {"conv": conv, "wu": nothing, "norm": nothing, "shift": nothing,
                                 "turn": turn, "select": select})

        @block.vector
        def _(dve):
            dve.memset(cw[0:D, 3:6, :], 0.0)
            dve.memset(seq[:, :, :, 0:XS:XS - 1].bitcast(F32), 0.0).then_inc(s["zero"], 1)

            def conv(i, p, n):
                dve.wait_ge(s["th"], at(i, CT, n + 1))
                if n == 0:
                    wait(dve, s["wu"], i, HG, 0)
                dve.scalar_tensor_tensor(xd2[:, n * CP:(n + 1) * CP], tc[:, n % 2, :], 1.0, ps_x[:, n % 2, 0:CP],
                                         ALU.add, ALU.mult).then_inc(s["xd"], 1)

            def stats(i, p, g):
                dve.wait_ge(s["x1"], at(i, HG, g + 1))
                wait(dve, s["sg"], i, NG, 2 * g)
                for a, c in enumerate((g, HG + g)):
                    dve.bn_stats(st[:, c, :], x1[:, p, c, :])
                    dve.tensor_tensor_reduce(junk[:, a, :], x1[:, p, c, :], k["gamma_r"][:, :], 1.0, 0.0, ALU.mult, ALU.add,
                                             gs[:, c:c + 1]).then_inc(s["sg"], 1)

            def wu(i, p, g):
                if g % 7 == 0:
                    dve.wait_ge(s["xb"], at(i, 2, g // 7 + 1))
                dve.wait_ge(s["wu"], at(i, HG, g + 1))
                dve.tensor_tensor(x1[:, p, g:NG:HG, :], ps_w[g % 2][0:GP, 0:2 * C].rearrange("p (a c) -> p a c", a=2),
                                  x1[:, p, g:NG:HG, :], ALU.add).then_inc(s["x1"], 1)
                if g:
                    stats(i, p, g - 1)

            def norm(i, p, h):
                if h:
                    stats(i, p, HG - 1)
                dve.wait_ge(s["sg"], at(i, NG, (2 * FIRST, NG)[h]))
                n0 = [5 * h]
                of = [st[:, :, c].rearrange("p (a g) -> p a g", a=2)[:, :, (0, FIRST)[h]:(FIRST, HG)[h]] for c in range(6)]

                def linked(op):
                    n0[0] += 1
                    op.then_inc(s["st"], 1)
                    dve.wait_ge(s["st"], at(i, 10, n0[0]))

                linked(dve.tensor_tensor(part(m_s, h), of[1], of[4], ALU.add))
                linked(dve.tensor_tensor(part(m_d, h), of[1], of[4], ALU.subtract))
                linked(dve.tensor_tensor(part(m_v, h), of[2], of[5], ALU.add))
                linked(dve.tensor_tensor(part(m_q, h), part(m_d, h), part(m_d, h), ALU.mult))
                linked(dve.tensor_scalar(part(m_v, h), part(m_v, h), 1.0 / C, EPS, ALU.mult, ALU.add))
                dve.scalar_tensor_tensor(part(var, h), part(m_q, h), 0.25, part(m_v, h), ALU.mult, ALU.add).then_inc(s["var"], 1)

            def shift(i, p, h):
                dve.wait_ge(s["rstd"], at(i, 2, h + 1))
                dve.scalar_tensor_tensor(part(nmr, h), part(m_s, h), -0.5, part(rstd, h), ALU.mult, ALU.mult).then_inc(s["nmr"], 1)
                if h:
                    dve.tensor_tensor(gr1[:, :], gs[:, :], rstd[:, :], ALU.mult).then_inc(s["gr1"], 1)
                    dve.wait_ge(s["nmr"], at(i, 2, 2))
                    dve.wait_ge(s["gr1"], at(i, 1, 1))
                    wait(dve, s["p1"], i, 1, 0)
                    dve.scalar_tensor_tensor(gray[:, :], nmr[:, :], k["gamma_sum"][:, :], gr1[:, :], ALU.mult, ALU.add).then_inc(s["gray"], 1)

            def turn(i, p, n):
                j, c = n // 2, n % 2
                dve.wait_ge(s["hi"], at(i, MT, n + 1))
                cs = slice(0, (128, C1)[c])
                high = unit_of(seq[cs, p, 2 * c, 1:1 + PIX], j)
                dve.tensor_tensor(unit_of(seq[C1 * c:128, p, 1 + c, 1:1 + PIX], j), tile_of(ps_x[cs, c, 0:TP]), high.bitcast(F32),
                                  ALU.subtract).then_inc(s["lo"], 1)

            def select(i, p, piece):
                if piece != 3:
                    return
                dve.wait_ge(s["p4"], at(i, 1, 1))
                dve.tensor_tensor(lgt[:, :], ps_s[0:1, 120:124], k["sel_b2"][:, :], ALU.add).then_inc(s["l1"], 1)
                dve.wait_ge(s["l1"], at(i, 1, 1))
                dve.tensor_tensor(cmp[:, 0:1], lgt[:, 1:2], lgt[:, 0:1], ALU.is_gt)
                dve.tensor_tensor(cmp[:, 1:2], lgt[:, 1:2], lgt[:, 2:3], ALU.is_ge)
                dve.tensor_tensor(cmp[:, 2:3], lgt[:, 1:2], lgt[:, 3:4], ALU.is_ge).then_inc(s["l2"], 1)
                dve.wait_ge(s["l2"], at(i, 1, 1))
                wait(dve, s["perm"], i, 1, 0)
                dve.scalar_tensor_tensor(flag[:, :], cmp[:, 0:1], cmp[:, 1:2], cmp[:, 2:3], ALU.mult, ALU.mult).then_inc(s["flag"], 1)

            def taps(i, p, n, m):
                r = n_par(i, p, n)
                dve.wait_ge(s["u"], at(i, MX, NB * n + m + 1))
                dve.scalar_tensor_tensor(u[:, r, m, :], ps_f[:, m, 0:TP], k["dw"][:, m, 0:1], u[:, r, m, :],
                                         ALU.mult, ALU.add).then_inc(s["w"], 1)
                dve.wait_ge(s["w"], at(i, MX, NB * n + m + 1))
                dve.scalar_tensor_tensor(u[:, r, m, :], ps_f[:, m, 2:TP + 2], k["dw"][:, m, 2:3], u[:, r, m, :],
                                         ALU.mult, ALU.add).then_inc(s["v"], 1)

            def out(i, p, n, q):
                step = 2 * n + q
                c = 2 * step
                dve.wait_ge(s["x1b"], at(i, NT, n + 1))
                dve.wait_ge(s["f2"], at(i, 2 * NT, step + 1))
                dve.tensor_tensor(x1[:, p, c:c + 2, :], ps_o[0:GP, 0:2 * C].rearrange("p (a c) -> p a c", a=2),
                                  x1[:, p, c:c + 2, :], ALU.add).then_inc(s["o"], 1)

            def slot(i, p, n, ahead, place):
                if n < NT:
                    taps(i, p, n, 0)
                place("A")
                if n < NT:
                    taps(i, p, n, 1)
                place("B")
                if n < NT:
                    taps(i, p, n, 2)
                place("C")
                if n:
                    out(i, p, n - 1, 0)
                place("D")
                if n:
                    out(i, p, n - 1, 1)
                place("E")

            schedule(dve, slot, {"conv": conv, "wu": wu, "norm": norm, "shift": shift, "turn": turn, "select": select})


def constants(np):
    diff = np.zeros((GP, 4, GP), np.float32)
    for m in range(GP):
        if m % W != W - 1:
            diff[m + 1, 0, m], diff[m, 0, m] = 1, -1
        if m < W:
            diff[m + W, 1, m], diff[m, 1, m] = 1, -1
        else:
            diff[m, 2, m] = -1
            diff[m - W, 3, m] = 1
    mixs = np.zeros((GP, 2, 4), np.float32)
    each = 1.0 / (C * H * (W - 1))
    mixs[:, 0, :] = [each, 0, 0.4 * each, each]
    mixs[:, 1, :] = [0, each, 0.4 * each, -each]
    return {"ident": np.eye(128, dtype=np.float32), "diff": diff, "mixs": mixs}


def kernel(**inputs):
    import numpy as np
    import concourse.bacc as bacc
    from concourse.bass_utils import run_bass_kernel_spmd

    a = {n: np.asarray(v) for n, v in inputs.items()}
    L0, L1 = "L0_conv_", "L1_conv_"
    col = lambda v: v.reshape(-1, 1)
    row = lambda v: v.reshape(1, -1)
    chan = lambda v: v.reshape(NB, 128).T
    laid = {
        "x": a["x"],
        "WdT0": a[L0 + "Wd"].T[0:128], "WdT1": a[L0 + "Wd"].T[128:], "W1T0": a[L0 + "W1"].T[0:128], "W1T1": a[L0 + "W1"].T[128:],
        "bd": col(a[L0 + "bd"]), "b1": col(a[L0 + "b1"]), "W2": a[L0 + "W2"], "W2T": a[L0 + "W2"].T, "b2": row(a[L0 + "b2"]),
        "tokT": a[L0 + "mask_token"].T, "WuT": a[L0 + "Wu"].T, "bu": row(a[L0 + "bu"]),
        "WhT": a[L0 + "Wh"].reshape(D, D, 9, D).transpose(3, 1, 2, 0).reshape(D, OC),
        "bh": a[L0 + "bh"].reshape(D, D, 9).transpose(1, 2, 0).reshape(1, OC),
        "fc1_0": a[L1 + "fc1_w"][0:128], "fc1_1": a[L1 + "fc1_w"][128:], "fc1_b": chan(a[L1 + "fc1_b"]),
        "gamma": row(a[L1 + "gamma"]), "gamma0": col(a[L1 + "gamma"])[0:128], "gamma1": col(a[L1 + "gamma"])[128:],
        "beta0": col(a[L1 + "beta"])[0:128], "beta1": col(a[L1 + "beta"])[128:],
        "dw_w": a[L1 + "dw_w"].reshape(NB, 128, 3).transpose(1, 0, 2), "dw_b": chan(a[L1 + "dw_b"]),
        "fc2_w": a[L1 + "fc2_w"].reshape(NB, 128, C).transpose(1, 0, 2), "fc2_b": row(a[L1 + "fc2_b"]),
        "sel_w1": a[L1 + "sel_w1"], "sel_b1": col(a[L1 + "sel_b1"]), "sel_w2": a[L1 + "sel_w2"], "sel_b2": row(a[L1 + "sel_b2"]),
        **constants(np),
    }
    nc = bacc.Bacc("TRN2", target_bir_lowering=False, num_devices=1)
    arrays, t = {}, {}
    for name, v in laid.items():
        arrays["in_" + name] = np.ascontiguousarray(v)
        t[name] = nc.dram_tensor("in_" + name, v.shape, F32, kind="ExternalInput").ap()
    out = nc.dram_tensor("out", (B, H, W, C), F32, kind="ExternalOutput").ap()
    t["map"] = nc.dram_tensor("map_scratch", (B, D, PADDED), F32, kind="Internal").ap()
    t["cw"] = nc.dram_tensor("cw_scratch", (B, OC), F32, kind="Internal").ap()
    t["cw_i"] = t["cw"].rearrange("b (c t d) -> b c t d", t=9, d=D)
    t["x_g"] = t["x"].rearrange("b (g r) w c -> b (r w) g c", r=2)
    t["out_g"] = out.rearrange("b (g r) w c -> b (r w) g c", r=2)
    build(nc, t)
    r = run_bass_kernel_spmd(nc, [arrays], core_ids=[0])
    return r.results[0]["out"]
```
